# Optimizing a Trainium2 kernel written in Bass

```python
import numpy as np
import jax
import jax.numpy as jnp

def _softmax(x, axis=-1):
    return jax.nn.softmax(x, axis=axis)

def _gelu(x):
    return jax.nn.gelu(x, approximate=True)

def _silu(x):
    return jax.nn.silu(x)

def _sigmoid(x):
    return jax.nn.sigmoid(x)

def _layernorm(x, axis=-1, eps=1e-05):
    m = jnp.mean(x, axis=axis, keepdims=True)
    v = jnp.var(x, axis=axis, keepdims=True)
    return (x - m) / jnp.sqrt(v + eps)

def _scatter_add(tgt, idx, src, axis=0):
    return tgt.at[idx].add(src)

def _segment_sum(src, seg, n):
    return jax.ops.segment_sum(src, seg, n)
kernel_name = 'mk_adj_preln_d1_adj_r2_a94aad'

def setup_inputs(seed: int=0):
    np.random.seed(seed)
    _w = jnp.asarray

    def _rec_inputs():
        import jax
        import jax.numpy as jnp
        _gk = jax.random.key(seed)
        x = 7.22e-05 + 1 * jax.random.normal(jax.random.fold_in(_gk, 1), (8, 1024, 512), jnp.float32)
        _a = jax.random.bernoulli(jax.random.fold_in(_gk, 2), 0.015625, (8, 1024, 1024))
        _a = jnp.logical_or(_a, jnp.swapaxes(_a, -1, -2))
        _a = jnp.logical_or(_a, jnp.eye(1024, dtype=bool))
        _af = _a.astype(jnp.float32)
        _af = _af * jax.random.uniform(jax.random.fold_in(_gk, 3), (8, 1024, 1024), jnp.float32, 0.05, 4.42607)
        adj = _af
        return (x, adj)
    x, adj = _rec_inputs()

    def _L0_gnn_setup():
        import jax, jax.numpy as jnp
        import numpy as np
        NUM_HEADS = 16
        key = jax.random.key(seed)
        ks = jax.random.split(key, 7)
        B, N, D = (16, 256, 512)
        return {'x': jax.random.normal(ks[0], (B, N, D), dtype=jnp.float32), 'spatial_encoding': jax.random.normal(ks[1], (B, N, N), dtype=jnp.float32), 'edge_encoding': jax.random.normal(ks[2], (B, N, N), dtype=jnp.float32), 'Wq': jax.random.normal(ks[3], (D, D), dtype=jnp.float32) * D ** (-0.5), 'Wk': jax.random.normal(ks[4], (D, D), dtype=jnp.float32) * D ** (-0.5), 'Wv': jax.random.normal(ks[5], (D, D), dtype=jnp.float32) * D ** (-0.5), 'Wo': jax.random.normal(ks[6], (D, D), dtype=jnp.float32) * D ** (-0.5)}
    _L0_gnn_all = _L0_gnn_setup()
    _L0_gnn_in = {k: v for k, v in _L0_gnn_all.items() if k in ('Wq', 'Wk', 'Wv', 'Wo')}
    del _L0_gnn_all
    return {'x': x, 'adj': adj, 'L0_gnn_Wq': _L0_gnn_in['Wq'], 'L0_gnn_Wk': _L0_gnn_in['Wk'], 'L0_gnn_Wv': _L0_gnn_in['Wv'], 'L0_gnn_Wo': _L0_gnn_in['Wo']}

def reference(x, adj, L0_gnn_Wq, L0_gnn_Wk, L0_gnn_Wv, L0_gnn_Wo):
    import jax
    import jax.numpy as jnp

    def _L0_gnn_ref(x, spatial_encoding, edge_encoding, Wq, Wk, Wv, Wo):
        import jax, jax.numpy as jnp
        import numpy as np
        NUM_HEADS = 16
        B, N, D = x.shape
        H = NUM_HEADS
        hd = D // H
        scale = D ** (-0.5)

        def split_heads(t):
            return t.reshape(B, N, H, hd).transpose(0, 2, 1, 3)
        q = split_heads(x @ Wq.T)
        k = split_heads(x @ Wk.T)
        v = split_heads(x @ Wv.T)
        bias = (spatial_encoding + edge_encoding)[:, None]
        a = jnp.einsum('bhnd,bhmd->bhnm', q, k) * scale + bias
        row_nonzero = jnp.any(a != 0, axis=-1, keepdims=True)
        a = jnp.where(row_nonzero, a, -jnp.inf)
        p = jax.nn.softmax(a, axis=-1)
        p = jnp.where(jnp.isnan(p), 0.0, p)
        o = jnp.einsum('bhnm,bhmd->bhnd', p, v)
        o = o.transpose(0, 2, 1, 3).reshape(B, N, D)
        return o @ Wo.T
    h = jnp.maximum(_layernorm(x, axis=-1), 0.0)
    x = x + _L0_gnn_ref(h, adj, adj, L0_gnn_Wq, L0_gnn_Wk, L0_gnn_Wv, L0_gnn_Wo)
    return x

_drawn_inputs = setup_inputs


def setup_inputs(seed=0):
    import zlib

    import numpy as np

    out = dict(_drawn_inputs(seed))
    spreads = {}
    factors = {'L0_gnn_Wq': 3.331, 'L0_gnn_Wk': 3.282}
    for name, (base, spread) in spreads.items():
        noise = np.random.default_rng([zlib.crc32(name.encode()), seed]).standard_normal(out[name].shape)
        drawn = base * np.exp(spread * noise) if base else spread * noise
        out[name] = jnp.asarray(drawn.astype(out[name].dtype))
    for name, factor in factors.items():
        out[name] = (out[name] * factor).astype(out[name].dtype)
    return out
```

```python
from contextlib import ExitStack

import numpy as np

import concourse.bass as bass
from concourse import mybir

ALU = mybir.AluOpType
ACT = mybir.ActivationFunctionType
AX = mybir.AxisListType
F32 = mybir.dt.float32
F32R = mybir.dt.float32r
I32 = mybir.dt.int32

P = 128
B, N, D, HEADS = 8, 1024, 512, 16
HD = D // HEADS
HPG = P // HD
G = HEADS // HPG
NT = N // P
MC = N // P
DC = D // P
HALF = N // 2
UPG = NT * HPG
U = G * UPG
PAIR = 2 * HPG
NP = U // PAIR
LEAF = 64
EPS = 1e-5
NEWTON = 3
RSQRT_BITS = float(0x5F3759DF)
QSCALE = float(D) ** -0.5 / 2.0
HI, LO = 0, 1
PRODUCTS = ((HI, HI), (HI, LO), (LO, HI))

PROJECT = ((2, "k", 0), (5, "k", 1), (18, "q", 0), (21, "q", 1),
           (23, "v", 0), (25, "vt", 0), (27, "v", 1), (29, "vt", 1))
SIDE = [(g * UPG + s, kind, g + 1, i) for g in range(G - 1) for s, kind, i in PROJECT]
LAST = (G - 1) * UPG
SIDE += [(LAST + 2 * t, "ln", G, t) for t in range(NT)]
SIDE += [(LAST + s, kind, G, i) for s, kind, i in (
    (15, "out", 0), (17, "k", 0), (18, "out", 1), (19, "k", 1), (21, "q", 0), (23, "q", 1),
    (25, "out", 2), (26, "out", 3), (30, "out", 4), (31, "out", 5))]
SIDE += [(U, kind, G, i) for kind, i in (
    ("v", 0), ("vt", 0), ("v", 1), ("vt", 1), ("out", 6), ("out", 7))]
SIDE += [(PAIR * (n + 1), "r", 0, n) for n in range(NP)]
SIDE.sort(key=lambda s: (s[0], s[1] != "r"))
FIRST = [(0, "ln", 0, t) for t in range(NT)] + [(0, kind, 0, i) for _, kind, i in PROJECT]
SPLIT = ("k", "q", "ln")
N_SIDE, N_FIRST = len(SIDE), len(FIRST)
N_SPLIT = sum(s[1] in SPLIT for s in SIDE)
N_FIRST_SPLIT = sum(s[1] in SPLIT for s in FIRST)
STACKS = 4 * HPG


def at_slot(slot):
    for n, (at, kind, g, i) in enumerate(SIDE):
        if at == slot:
            yield n, sum(t[1] in SPLIT for t in SIDE[:n]), kind, g, i


def first_pieces():
    for n, (_, kind, g, i) in enumerate(FIRST):
        yield n, sum(t[1] in SPLIT for t in FIRST[:n]), kind, g, i


def number(kind, g, i):
    return next(n for n, s in enumerate(SIDE) if s[1:] == (kind, g, i))


def unit(u):
    g, s = divmod(u, UPG)
    return g, s // HPG, s % HPG


WEIGHTS = ("k", "q", "v")


def weight_load(kind, g):
    return len(WEIGHTS) * g + WEIGHTS.index(kind)


def adj_attention_block(nc, x, adj, wq, wk, wv, wo, y):
    with ExitStack() as ctx:
        def sb(name, shape, dt=F32):
            return ctx.enter_context(nc.sbuf_tensor(name, shape, dt))

        def sem(name):
            return ctx.enter_context(nc.semaphore(name))

        w_split = nc.dram_tensor("w_split", [3, G, P, 2 * DC * P], F32, kind="Internal").ap()
        o_split = nc.dram_tensor("o_split", [2, G, P, N], F32, kind="Internal").ap()

        ident = sb("ident", [P, P])
        hT = [sb("hT_hi", [P, DC, N], F32R), sb("hT_lo", [P, DC, N], F32R)]
        w_proj = sb("w_proj", [P, 2, 2, DC, P], F32R)
        w_out = sb("w_out", [P, 2, DC, D], F32R)
        qf = sb("qf", [P, 2, HALF], F32R)
        kf = sb("kf", [P, 2, HALF], F32R)
        vTh = sb("vTh", [P, HALF])
        q_stack = sb("q_stack", [P, HPG, N], F32R)
        k_stack = sb("k_stack", [P, 2, HPG, N], F32R)
        v_sb = sb("v_sb", [P, 2, MC, P])
        adj_sb = sb("adj_sb", [P, 2, N])
        neg_a = sb("neg_a", [P, 2, N])
        prob = sb("prob", [P, 2, N])
        probT = sb("probT", [P, HPG, MC, 2 * P])
        x_ln = sb("x_ln", [P, 2, D])
        x_res = sb("x_res", [P, 2, D])
        o_norm = sb("o_norm", [P, 2 * P])
        recT = sb("recT", [P, 2 * P])
        o_hl = sb("o_hl", [P, 2, 2 * P], F32R)
        o_in = sb("o_in", [P, 2, 2, G, P], F32R)
        tree = sb("tree", [P, 512 + 256 + 128])
        leaf = sb("leaf", [P, 2, PAIR, LEAF])
        neg_max = sb("neg_max", [P, 2, PAIR])
        neg_sum = sb("neg_sum", [P, PAIR])
        nonzero = sb("nonzero", [P, PAIR])
        rec_sum = sb("rec_sum", [P, PAIR])
        rec = sb("rec", [P, PAIR])
        row_sum = sb("row_sum", [P, 2, PAIR])
        rec_rep = sb("rec_rep", [P, 2, HPG, HD])
        bn = sb("bn", [P, 6])
        mean_var = sb("mean_var", [P, 2])
        var_eps, rstd, newton = sb("var_eps", [P, 1]), sb("rstd", [P, 1]), sb("newton", [P, 1])

        ps = ctx.enter_context(nc.psum_tensor("ps", [P, 8, HALF], F32))
        side = ps[:, 7, :]
        heads_out = ps[:, 6, 0:2 * P]

        s_apart = sem("waits_carried_apart")
        s_zero, s_ident = sem("ident_zeroed"), sem("ident_ready")
        s_wload = [sem(f"weights_loaded_{i}") for i in range(4)]
        s_wt, s_whi, s_wlo = sem("weights_turned"), sem("weights_hi"), sem("weights_lo")
        s_wst = sem("weights_stored")
        s_adj = [sem("adj_loaded_0"), sem("adj_loaded_1")]
        s_x = [sem("x_ln_loaded_0"), sem("x_ln_loaded_1")]
        s_xr = [sem("x_res_loaded_0"), sem("x_res_loaded_1")]
        s_wp = [sem("w_proj_loaded_0"), sem("w_proj_loaded_1")]
        s_oin = [sem("o_in_loaded_0"), sem("o_in_loaded_1")]
        s_kst = sem("k_stacked")
        s_qst = [sem("q_stacked_0"), sem("q_stacked_1")]
        s_qk, s_max, s_exp = sem("scores_ready"), sem("max_ready"), sem("probs_ready")
        s_tree1, s_leaf = sem("scores_read_by_gpsimd"), sem("leaf_ready")
        s_tree = sem("tree_step")
        s_turn = sem("probs_turned")
        s_copy = [sem("first_half_copied"), sem("second_half_copied")]
        s_rr, s_rstep = sem("rec_rep_ready"), sem("rec_step")
        s_pv = sem("heads_ready")
        s_norm, s_ohi, s_olo = sem("o_norm_ready"), sem("o_hi_ready"), sem("o_lo_ready")
        s_ost = sem("o_stored")
        s_piece, s_hi, s_evac = sem("piece_ready"), sem("piece_hi"), sem("piece_evacuated")
        s_bn, s_mv, s_ve, s_guess = sem("bn_ready"), sem("mean_var_ready"), sem("var_eps_ready"), sem("rstd_guessed")
        s_newton, s_xn = sem("newton_step"), sem("xn_ready")
        s_y = [sem("y_stored_0"), sem("y_stored_1")]

        w_dram = (wk, wq, wv, wo)
        w_stage = [hT[0][:].rearrange("p c (h e) -> p (c h) e", h=2), hT[1][:].rearrange("p c (h e) -> p (c h) e", h=2),
                   k_stack[:, 0].rearrange("p c (h e) -> p (c h) e", h=2), w_out[:].rearrange("p s c e -> p (s c) e")]
        w_raw = probT[:].rearrange("p h c n -> p (h c n)").rearrange("p (w o d) -> p w o d", w=4, o=DC)

        block = ctx.enter_context(nc.Block())


        def pieces_before(b):
            return 0 if b is None else N_FIRST + b * N_SIDE

        def splits_before(b):
            return 0 if b is None else N_FIRST_SPLIT + b * N_SPLIT

        def groups_before(b):
            return 0 if b is None else b * G

        def norms_before(b):
            return 0 if b is None else NT + b * NT

        def apart(eng):
            eng.sem_inc(s_apart, 1)

        @block.sync
        def _(sp):
            def load_weights(load):
                g, which = divmod(load, len(WEIGHTS))
                sp.dma_start(w_proj[:, load % 2].rearrange("p s c e -> p (s c e)").bitcast(F32),
                             w_split[which, g % G]).then_inc(s_wp[load % 2], 16)

            def stack(kind, g, half):
                cols = slice(half * HALF, (half + 1) * HALF)
                for h in range(HPG):
                    dims = slice(h * HD, (h + 1) * HD)
                    for r in range(4):
                        rows = slice(r * HD, (r + 1) * HD)
                        if kind == "k":
                            sp.dma_start(k_stack[rows, g % 2, h, cols].bitcast(F32),
                                         kf[dims, r % 2, :].bitcast(F32)).then_inc(s_kst, 16)
                        else:
                            sp.dma_start(q_stack[rows, h, cols].bitcast(F32),
                                         qf[dims, r // 2, :].bitcast(F32)).then_inc(s_qst[half], 16)

            def load_x(b, t):
                sp.dma_start(x_ln[:, t % 2, :], x[b, t * P:(t + 1) * P, :]).then_inc(s_x[t % 2], 16)

            def load_adj(b, t):
                sp.dma_start(adj_sb[:, t % 2, :], adj[b, t * P:(t + 1) * P, :]).then_inc(s_adj[t % 2], 16)

            def store_heads(b, n):
                cols = slice((n % 4) * 2 * P, (n % 4 + 1) * 2 * P)
                sp.wait_ge(s_ohi, b * NP + n + 1)
                apart(sp)
                sp.wait_ge(s_olo, b * NP + n + 1)
                apart(sp)
                sp.dma_start(o_split[:, n // 4, :, cols].rearrange("s p n -> p s n"),
                             o_hl[:].bitcast(F32)).then_inc(s_ost, 16)

            def load_out_inputs(b, t):
                rows = slice(t * P, (t + 1) * P)
                if t >= 2:
                    sp.wait_ge(s_y[t % 2], 16 * (b * (NT // 2) + t // 2))
                    apart(sp)
                sp.dma_start(x_res[:, t % 2, :], x[b, rows, :]).then_inc(s_xr[t % 2], 16)
                sp.wait_ge(s_ost, 16 * (b * NP + (G - 1) * 4 + t // 2 + 1))
                apart(sp)
                for part in (HI, LO):
                    sp.dma_start(o_in[:, t % 2, part].bitcast(F32), o_split[part, :, :, rows].rearrange("g p n -> p g n")
                                 ).then_inc(s_oin[t % 2], 16)

            def after_piece(b, xb, n, kind, g, i):
                done = pieces_before(b) + n + 1
                if kind == "ln" and i + 2 < NT:
                    sp.wait_ge(s_piece, done)
                    apart(sp)
                    load_x(xb, i + 2)
                if kind == "k" or (kind == "q" and (i == 0 or b is None)):
                    if b is not None and kind == "q":
                        sp.wait_ge(s_qk, b * U + (g - 1) * UPG + UPG // 2)
                        apart(sp)
                    sp.wait_ge(s_evac, done)
                    apart(sp)
                    stack(kind, g, i)
                if kind in WEIGHTS and i == 1:
                    sp.wait_ge(s_piece, done)
                    apart(sp)
                    load_weights(weight_load(kind, g) + 2)
                if kind == "out":
                    sp.wait_ge(s_evac, done)
                    apart(sp)
                    sp.dma_start(y[b, i * P:(i + 1) * P, :], x_res[:, i % 2, :]).then_inc(s_y[i % 2], 16)

            for i, w in enumerate(w_dram):
                sp.dma_start(w_raw[:, i], w.rearrange("(o p) d -> p o d", p=P)).then_inc(s_wload[i], 16)
            load_x(0, 0)
            load_x(0, 1)
            load_adj(0, 0)
            for i in range(len(WEIGHTS)):
                sp.wait_ge(s_whi, DC * (i + 1))
                sp.wait_ge(s_wlo, DC * (i + 1))
                for g in range(G):
                    sp.dma_start(w_split[i, g].rearrange("p (s e) -> p s e", e=P),
                                 w_stage[i][:, :, g * P:(g + 1) * P].bitcast(F32)).then_inc(s_wst, 16)
            sp.wait_ge(s_wst, 16 * len(WEIGHTS) * G)
            load_weights(0)
            load_weights(1)
            for n, _, kind, g, i in first_pieces():
                after_piece(None, 0, n, kind, g, i)

            with sp.Fori(0, B) as b:
                nb = (b + 1) % B
                for u in range(U):
                    g, s = divmod(u, UPG)
                    if s % HPG == 0:
                        t = u // HPG + 1
                        if u:
                            sp.wait_ge(s_max, b * U + u)
                            apart(sp)
                        load_adj(b if t < NT * G else nb, t % NT)
                    if u > 0:
                        for n, _, kind, pg, i in at_slot(u - 1):
                            after_piece(b, nb, n, kind, pg, i)
                    if s == UPG - 1:
                        sp.wait_ge(s_qk, b * U + (g + 1) * UPG)
                        apart(sp)
                        sp.wait_ge(s_evac, pieces_before(b) + number("q", g + 1, 1) + 1)
                        apart(sp)
                        stack("q", g + 1, 1)
                    if u >= PAIR + 3 and (u - 3) % PAIR == 0:
                        store_heads(b, (u - 3) // PAIR - 1)
                    if u in (LAST - 4, LAST - 3):
                        load_x(nb, u - LAST + 4)
                    for t, at in ((0, 12), (1, 12), (2, 20), (3, 21), (4, 28), (5, 29)):
                        if u == LAST + at:
                            load_out_inputs(b, t)
                for n, _, kind, pg, i in at_slot(U - 1):
                    after_piece(b, nb, n, kind, pg, i)
                store_heads(b, NP - 1)
                load_out_inputs(b, NT - 2)
                load_out_inputs(b, NT - 1)
                for n, _, kind, pg, i in at_slot(U):
                    after_piece(b, nb, n, kind, pg, i)
                for i in range(2):
                    sp.wait_ge(s_y[i], 16 * (b * (NT // 2) + NT // 2))
                    apart(sp)

            for i in range(2):
                sp.wait_ge(s_y[i], 16 * B * NT // 2)
                apart(sp)
                sp.wait_ge(s_wp[i], 16 * (B * G * len(WEIGHTS) // 2 + (3 if i == 0 else 2)))
                apart(sp)
            sp.wait_ge(s_adj[0], 16 * (B * G * NT // 2 + 1))
            apart(sp)

        @block.gpsimd
        def _(pool):
            def rstd_of(k):
                pool.wait_ge(s_guess, k + 1)
                for step in range(NEWTON):
                    done = (k * NEWTON + step) * 4
                    pool.tensor_tensor(newton[:], rstd[:], rstd[:], ALU.mult).then_inc(s_newton, 1)
                    pool.wait_ge(s_newton, done + 1)
                    pool.tensor_tensor(newton[:], newton[:], var_eps[:], ALU.mult).then_inc(s_newton, 1)
                    pool.wait_ge(s_newton, done + 2)
                    apart(pool)
                    pool.tensor_scalar(newton[:], newton[:], -0.5, 1.5, ALU.mult, ALU.add).then_inc(s_newton, 1)
                    pool.wait_ge(s_newton, done + 3)
                    pool.tensor_tensor(rstd[:], rstd[:], newton[:], ALU.mult).then_inc(s_newton, 1)
                    if step + 1 < NEWTON:
                        pool.wait_ge(s_newton, done + 4)

            pool.memset(ident[:], 0.0).then_inc(s_zero, 1)
            pool.wait_ge(s_zero, 1)
            pool.affine_select(out=ident[:], in_=ident[:], compare_op=ALU.not_equal, fill=1.0, base=0,
                               pattern=[[-1, P]], channel_multiplier=1).then_inc(s_ident, 1)
            for t in range(NT):
                rstd_of(t)

            with pool.Fori(0, B) as b:
                for u in range(U):
                    n = u // PAIR
                    done = b * U + u
                    pool.wait_ge(s_max, done + 1)
                    pool.tensor_tensor(tree[:, 0:512], neg_a[:, u % 2, 0:512], neg_a[:, u % 2, 512:1024],
                                       ALU.add).then_inc(s_tree1, 1)
                    pool.wait_ge(s_tree1, done + 1)
                    pool.tensor_tensor(tree[:, 512:768], tree[:, 0:256], tree[:, 256:512],
                                       ALU.add).then_inc(s_tree, 1)
                    pool.wait_ge(s_tree, done * 2 + 1)
                    pool.tensor_tensor(tree[:, 768:896], tree[:, 512:640], tree[:, 640:768],
                                       ALU.add).then_inc(s_tree, 1)
                    pool.wait_ge(s_tree, done * 2 + 2)
                    pool.tensor_tensor(leaf[:, n % 2, u % PAIR, :], tree[:, 768:832], tree[:, 832:896],
                                       ALU.add).then_inc(s_leaf, 1)
                    if u >= LAST - 1 and (u - LAST) % 2 and (u - LAST + 1) // 2 < NT:
                        rstd_of(norms_before(b) + (u - LAST + 1) // 2)

        @block.tensor
        def _(pe):
            def scores(b, u):
                g, t, h = unit(u)
                if u >= 2:
                    pe.wait_ge(s_max, b * U + u - 1)
                if u % UPG == 0:
                    pe.wait_ge(s_kst, 16 * 2 * STACKS * (b * G + g + 1))
                    pe.wait_ge(s_qst[0], 16 * STACKS * (b * G + g + 1))
                if u % UPG == UPG // 2:
                    pe.wait_ge(s_qst[1], 16 * STACKS * (b * G + g + 1))
                for half in range(2):
                    mm = pe.matmul(ps[:, 2 * (u % 2) + half, :], q_stack[:, h, t * P:(t + 1) * P],
                                   k_stack[:, g % 2, h, half * HALF:(half + 1) * HALF], start=True, stop=True)
                mm.then_inc(s_qk, 1)

            def turn_probs(b, u):
                pe.wait_ge(s_exp, b * U + u + 1)
                for half in range(2):
                    if u:
                        pe.wait_ge(s_copy[half], b * U + u)
                    for c in range(4):
                        mm = pe.transpose(ps[:, 4 + half, c * P:(c + 1) * P],
                                          prob[:, u % 2, (4 * half + c) * P:(4 * half + c + 1) * P], ident[:])
                    mm.then_inc(s_turn, 1)

            def times_v(b, n):
                g = n // 4
                if n:
                    pe.wait_ge(s_norm, b * NP + n)
                pe.wait_ge(s_copy[0], b * U + PAIR * (n + 1))
                pe.wait_ge(s_copy[1], b * U + PAIR * (n + 1))
                pe.wait_ge(s_evac, pieces_before(b) + (number("vt", g, 1) + 1 if g else 0))
                for c in range(MC):
                    for h in range(HPG):
                        mm = pe.matmul(ps[h * HD:(h + 1) * HD, 6, 0:2 * P], v_sb[:, g % 2, c, h * HD:(h + 1) * HD],
                                       probT[:, h, c, :], start=(c == 0), stop=(c == MC - 1))
                mm.then_inc(s_pv, 1)

            def piece(b, n, kind, g, i):
                if n or b is not None:
                    pe.wait_ge(s_evac, pieces_before(b) + n)
                if kind in WEIGHTS:
                    load = weight_load(kind, g)
                    if i == 0:
                        loads = 0 if b is None else b * (G * len(WEIGHTS) // 2)
                        pe.wait_ge(s_wp[load % 2], 16 * (loads + load // 2 + 1))
                    for k, (c, (pw, ph)) in enumerate((c, p) for c in range(DC) for p in PRODUCTS):
                        mm = pe.matmul(side, w_proj[:, load % 2, pw, c, :], hT[ph][:, c, i * HALF:(i + 1) * HALF],
                                       start=(k == 0), stop=(k == DC * len(PRODUCTS) - 1))
                elif kind == "vt":
                    for c in range(4):
                        mm = pe.transpose(side[:, c * P:(c + 1) * P], vTh[:, c * P:(c + 1) * P], ident[:])
                elif kind == "ln":
                    pe.wait_ge(s_xn, norms_before(b) + i + 1)
                    for c in range(DC):
                        mm = pe.transpose(side[:, c * P:(c + 1) * P], x_ln[:, i % 2, c * P:(c + 1) * P], ident[:])
                elif kind == "r":
                    pe.wait_ge(s_rr, b * NP + i + 1)
                    for j in range(2):
                        mm = pe.transpose(side[:, j * P:(j + 1) * P],
                                          rec_rep[:, j].rearrange("p h d -> p (h d)"), ident[:])
                else:
                    pe.wait_ge(s_oin[i % 2], 32 * (b * (NT // 2) + i // 2 + 1))
                    for k, (c, (po, pw)) in enumerate((c, p) for c in range(G) for p in PRODUCTS):
                        mm = pe.matmul(side, o_in[:, i % 2, po, c, :], w_out[:, pw, c, :],
                                       start=(k == 0), stop=(k == G * len(PRODUCTS) - 1))
                mm.then_inc(s_piece, 1)

            pe.wait_ge(s_ident, 1)
            for k in range(4 * DC):
                w, ic = divmod(k, DC)
                if ic == 0:
                    pe.wait_ge(s_wload[w], 16)
                if k >= 4:
                    pe.wait_ge(s_wlo, k - 3)
                for oc in range(DC):
                    mm = pe.transpose(ps[:, k % 4, oc * P:(oc + 1) * P],
                                      w_raw[:, w, oc, ic * P:(ic + 1) * P], ident[:])
                mm.then_inc(s_wt, 1)
            pe.wait_ge(s_wlo, 4 * DC)
            for n, _, kind, g, i in first_pieces():
                piece(None, n, kind, g, i)

            with pe.Fori(0, B) as b:
                scores(b, 0)
                scores(b, 1)
                for u in range(U):
                    if u + 2 < U:
                        scores(b, u + 2)
                    turn_probs(b, u)
                    if u and u % PAIR == 0:
                        times_v(b, u // PAIR - 1)
                    for n, _, kind, g, i in at_slot(u):
                        piece(b, n, kind, g, i)
                times_v(b, NP - 1)
                for n, _, kind, g, i in at_slot(U):
                    piece(b, n, kind, g, i)

        @block.scalar
        def _(act):
            def probs(b, u):
                n = u // PAIR
                act.wait_ge(s_max, b * U + u + 1)
                if u >= 2:
                    act.wait_ge(s_turn, (b * U + u - 1) * 2)
                act.activation(prob[:, u % 2, :], neg_a[:, u % 2, :], ACT.Exp,
                               bias=neg_max[:, n % 2, u % PAIR:u % PAIR + 1], scale=-1.0,
                               accum_out=row_sum[:, n % 2, u % PAIR:u % PAIR + 1]).then_inc(s_exp, 1)

            def copy_turned(b, u):
                _, t, h = unit(u)
                act.wait_ge(s_turn, (b * U + u) * 2 + 1)
                if u >= PAIR:
                    act.wait_ge(s_pv, b * NP + u // PAIR)
                act.copy(probT[:, h, 0:4, (t % 2) * P:(t % 2 + 1) * P],
                         ps[:, 4, :].rearrange("p (c n) -> p c n", n=P)).then_inc(s_copy[0], 1)

            def split_hi(b, n, m, kind, g, i):
                if kind not in SPLIT:
                    return
                act.wait_ge(s_piece, pieces_before(b) + n + 1)
                if kind == "k":
                    if b is not None or i:
                        act.wait_ge(s_kst, 16 * STACKS * (groups_before(b) * 2 + 2 * g + i))
                    act.copy(kf[:, HI, :], side).then_inc(s_hi, 1)
                elif kind == "q":
                    if b is not None or i:
                        act.wait_ge(s_qst[1 - i], 16 * STACKS * (groups_before(b) + g + i))
                    act.mul(qf[:, HI, :], side, QSCALE).then_inc(s_hi, 1)
                else:
                    act.activation(hT[HI][:, :, i * P:(i + 1) * P], side.rearrange("p (c n) -> p c n", n=P),
                                   ACT.Relu).then_inc(s_hi, 1)

            def heads_hi(b, n):
                act.wait_ge(s_norm, b * NP + n + 1)
                if n:
                    act.wait_ge(s_ost, 16 * (b * NP + n))
                act.copy(o_hl[:, HI, :], o_norm[:]).then_inc(s_ohi, 1)

            for k in range(4 * DC):
                w, ic = divmod(k, DC)
                act.wait_ge(s_wt, k + 1)
                act.copy(w_stage[w][:, HI * DC + ic, :], ps[:, k % 4, :]).then_inc(s_whi, 1)
            act.wait_ge(s_wst, 16 * len(WEIGHTS) * G)
            for n, m, kind, g, i in first_pieces():
                split_hi(None, n, m, kind, g, i)

            with act.Fori(0, B) as b:
                probs(b, 0)
                for u in range(U):
                    if u + 1 < U:
                        probs(b, u + 1)
                    if u:
                        for n, m, kind, g, i in at_slot(u - 1):
                            split_hi(b, n, m, kind, g, i)
                    copy_turned(b, u)
                    if u > PAIR and u % PAIR == 1:
                        heads_hi(b, u // PAIR - 1)
                heads_hi(b, NP - 1)
                for n, m, kind, g, i in at_slot(U):
                    split_hi(b, n, m, kind, g, i)

        @block.vector
        def _(dve):
            def bias_and_max(b, u):
                _, t, _ = unit(u)
                n = u // PAIR
                tile = u // HPG
                dve.wait_ge(s_qk, b * U + u + 1)
                if u % HPG == 0:
                    dve.wait_ge(s_adj[tile % 2], 16 * (b * (G * NT // 2) + tile // 2 + 1))
                if u >= 2:
                    dve.wait_ge(s_exp, b * U + u - 1)
                    dve.wait_ge(s_tree1, b * U + u - 1)
                apart(dve)
                dve.tensor_tensor_reduce(
                    neg_a[:, u % 2, :], ps[:, 2 * (u % 2):2 * (u % 2) + 2, :].rearrange("p h m -> p (h m)"),
                    adj_sb[:, tile % 2, :], -2.0, 3.0e38, ALU.add, ALU.min,
                    neg_max[:, n % 2, u % PAIR:u % PAIR + 1]).then_inc(s_max, 1)

            def copy_turned(b, u):
                _, t, h = unit(u)
                dve.wait_ge(s_turn, (b * U + u) * 2 + 2)
                if u >= PAIR:
                    dve.wait_ge(s_pv, b * NP + u // PAIR)
                dve.tensor_copy(probT[:, h, 4:8, (t % 2) * P:(t % 2 + 1) * P],
                                ps[:, 5, :].rearrange("p (c n) -> p c n", n=P)).then_inc(s_copy[1], 1)

            def reciprocals(b, n):
                steps = (b * NP + n) * 5
                dve.wait_ge(s_leaf, b * U + PAIR * (n + 1))
                dve.wait_ge(s_exp, b * U + PAIR * (n + 1))
                dve.tensor_reduce(neg_sum[:], leaf[:, n % 2], AX.X, ALU.add).then_inc(s_rstep, 1)
                dve.reciprocal(rec_sum[:], row_sum[:, n % 2]).then_inc(s_rstep, 1)
                dve.tensor_scalar(nonzero[:], neg_max[:, n % 2], 0.0, None, ALU.not_equal).then_inc(s_rstep, 1)
                dve.wait_ge(s_rstep, steps + 3)
                dve.scalar_tensor_tensor(nonzero[:], neg_sum[:], 0.0, nonzero[:], ALU.not_equal, ALU.max
                                         ).then_inc(s_rstep, 1)
                dve.wait_ge(s_rstep, steps + 4)
                dve.tensor_tensor(rec[:], nonzero[:], rec_sum[:], ALU.mult).then_inc(s_rstep, 1)
                dve.wait_ge(s_rstep, steps + 5)
                dve.tensor_copy(rec_rep[:].rearrange("p j h d -> p (j h) d"),
                                rec[:].unsqueeze(2).to_broadcast([P, PAIR, HD])).then_inc(s_rr, 1)

            def tile_stats(b, t):
                k = norms_before(b) + t
                loads = (t // 2 + 1) if b is None else (b * (NT // 2) + NT // 2 + t // 2 + 1)
                dve.wait_ge(s_x[t % 2], 16 * loads)
                dve.bn_stats(bn[:], x_ln[:, t % 2, :]).then_inc(s_bn, 1)
                dve.wait_ge(s_bn, k + 1)
                apart(dve)
                dve.bn_aggr(mean_var[:], bn[:]).then_inc(s_mv, 1)
                dve.wait_ge(s_mv, k + 1)
                dve.tensor_scalar(var_eps[:], mean_var[:, 1:2], EPS, None, ALU.add).then_inc(s_ve, 1)
                dve.wait_ge(s_ve, k + 1)
                dve.tensor_scalar(rstd[:].bitcast(I32), var_eps[:].bitcast(I32), -0.5, RSQRT_BITS,
                                  ALU.mult, ALU.add).then_inc(s_guess, 1)

            def tile_norm(b, t):
                k = norms_before(b) + t
                dve.wait_ge(s_newton, (k + 1) * NEWTON * 4)
                dve.tensor_scalar(x_ln[:, t % 2, :], x_ln[:, t % 2, :], mean_var[:, 0:1], rstd[:, 0:1],
                                  ALU.subtract, ALU.mult).then_inc(s_xn, 1)

            def evacuate(b, n, m, kind, g, i):
                dve.wait_ge(s_piece, pieces_before(b) + n + 1)
                if kind in SPLIT:
                    dve.wait_ge(s_hi, splits_before(b) + m + 1)
                side_c = side.rearrange("p (c n) -> p c n", n=P)
                if kind == "k":
                    op = dve.scalar_tensor_tensor(kf[:, LO, :], side, 1.0, kf[:, HI, :].bitcast(F32),
                                                  ALU.mult, ALU.subtract)
                elif kind == "q":
                    op = dve.scalar_tensor_tensor(qf[:, LO, :], side, QSCALE, qf[:, HI, :].bitcast(F32),
                                                  ALU.mult, ALU.subtract)
                elif kind == "ln":
                    rows = slice(i * P, (i + 1) * P)
                    op = dve.scalar_tensor_tensor(hT[LO][:, :, rows], side_c, 0.0, hT[HI][:, :, rows].bitcast(F32),
                                                  ALU.max, ALU.subtract)
                elif kind == "v":
                    op = dve.tensor_copy(vTh[:], side)
                elif kind == "vt":
                    op = dve.tensor_copy(v_sb[:, g % 2, 4 * i:4 * i + 4, :], side_c)
                elif kind == "r":
                    op = dve.tensor_copy(recT[:], side[:, 0:2 * P])
                else:
                    dve.wait_ge(s_xr[i % 2], 16 * (b * (NT // 2) + i // 2 + 1))
                    op = dve.tensor_tensor(x_res[:, i % 2, :], side, x_res[:, i % 2, :], ALU.add)
                op.then_inc(s_evac, 1)
                if kind == "r":
                    dve.wait_ge(s_pv, b * NP + i + 1)
                    dve.wait_ge(s_evac, pieces_before(b) + n + 1)
                    dve.tensor_tensor(o_norm[:], heads_out, recT[:], ALU.mult).then_inc(s_norm, 1)

            def heads_lo(b, n):
                dve.wait_ge(s_ohi, b * NP + n + 1)
                dve.tensor_tensor(o_hl[:, LO, :], o_norm[:], o_hl[:, HI, :].bitcast(F32), ALU.subtract
                                  ).then_inc(s_olo, 1)

            for k in range(4 * DC):
                w, ic = divmod(k, DC)
                dve.wait_ge(s_whi, k + 1)
                dve.scalar_tensor_tensor(w_stage[w][:, LO * DC + ic, :], ps[:, k % 4, :], 1.0,
                                         w_stage[w][:, HI * DC + ic, :].bitcast(F32),
                                         ALU.mult, ALU.subtract).then_inc(s_wlo, 1)
            dve.wait_ge(s_wst, 16 * len(WEIGHTS) * G)
            for n, m, kind, g, i in first_pieces():
                if kind == "ln":
                    tile_stats(None, i)
                    tile_norm(None, i)
                evacuate(None, n, m, kind, g, i)

            with dve.Fori(0, B) as b:
                bias_and_max(b, 0)
                for u in range(U):
                    if u + 1 < U:
                        bias_and_max(b, u + 1)
                    if u % PAIR == 2 and u > PAIR:
                        heads_lo(b, u // PAIR - 1)
                    if u:
                        for n, m, kind, g, i in at_slot(u - 1):
                            evacuate(b, n, m, kind, g, i)
                    if u >= LAST and (u - LAST) % 2 == 0 and (u - LAST) // 2 < NT:
                        tile_norm(b, (u - LAST) // 2)
                    copy_turned(b, u)
                    if u and u % PAIR == 0:
                        reciprocals(b, u // PAIR - 1)
                    if u >= LAST - 1 and (u - LAST) % 2 and (u - LAST + 1) // 2 < NT:
                        tile_stats(b, (u - LAST + 1) // 2)
                reciprocals(b, NP - 1)
                for n, m, kind, g, i in at_slot(U - 1):
                    evacuate(b, n, m, kind, g, i)
                for n, m, kind, g, i in at_slot(U):
                    evacuate(b, n, m, kind, g, i)
                    if kind == "r":
                        heads_lo(b, NP - 1)


_INS = ["x", "adj", "L0_gnn_Wq", "L0_gnn_Wk", "L0_gnn_Wv", "L0_gnn_Wo"]


def kernel(**inputs):
    import concourse.bacc as bacc
    from concourse.bass_utils import run_bass_kernel_spmd

    nc = bacc.Bacc("TRN2", target_bir_lowering=False, num_devices=1)
    arrays, args = {}, []
    for name in _INS:
        a = np.ascontiguousarray(inputs[name])
        arrays[f"in_{name}"] = a
        args.append(nc.dram_tensor(f"in_{name}", a.shape, mybir.dt.from_np(a.dtype), kind="ExternalInput").ap())
    out = nc.dram_tensor("out_y", (B, N, D), F32, kind="ExternalOutput").ap()
    adj_attention_block(nc, *args, out)
    r = run_bass_kernel_spmd(nc, [arrays], core_ids=[0])
    return r.results[0]["out_y"]
```

```python
from contextlib import ExitStack

import numpy as np

import concourse.bass as bass
from concourse import mybir

ALU = mybir.AluOpType
ACT = mybir.ActivationFunctionType
AX = mybir.AxisListType
F32 = mybir.dt.float32
F32R = mybir.dt.float32r
I32 = mybir.dt.int32

P = 128
B, N, D, HEADS = 8, 1024, 512, 16
HD = D // HEADS
HPG = P // HD
G = HEADS // HPG
NT = N // P
MC = N // P
DC = D // P
HALF = N // 2
UPG = NT * HPG
U = G * UPG
PAIR = 2 * HPG
NP = U // PAIR
LEAF = 128
EPS = 1e-5
NEWTON = 3
RSQRT_BITS = float(0x5F3759DF)
QSCALE = float(D) ** -0.5 / 2.0
HI, LO = 0, 1
PRODUCTS = ((HI, HI), (HI, LO), (LO, HI))

PROJECT_QK = (("k", 0), ("q", 0), ("k", 1), ("q", 1))
PROJECT_V = (("v", 0), ("vt", 0), ("v", 1), ("vt", 1))
SIDE = [(s, kind, 0, i) for s, (kind, i) in zip((2, 4, 5, 7), PROJECT_V)]
SIDE += [(g * UPG + s, kind, g + 1, i) for g in range(G - 1)
         for s, (kind, i) in zip((10, 14, 18, 21, 23, 25, 27, 29), PROJECT_QK + PROJECT_V)]
LAST = (G - 1) * UPG
SIDE += [(LAST + 2 * t + 1, "ln", G, t) for t in range(NT)]
SIDE += [(LAST + s, kind, G, i) for s, kind, i in (
    (18, "k", 0), (19, "out", 0), (20, "out", 1), (21, "q", 0), (23, "k", 1), (26, "out", 2),
    (27, "q", 1), (28, "out", 3), (31, "out", 4))]
SIDE += [(U, "out", G, i) for i in (5, 6, 7)]
LEAD = 2
SIDE += [(PAIR * (n + 1), "r", 0, n) for n in range(NP)]
SIDE.sort(key=lambda s: (s[0], s[1] != "r"))
assert all(sum(s[0] == u for s in SIDE) <= 1 for u in range(U))
FIRST = [(0, "ln", 0, t) for t in range(NT)] + [(0, kind, 0, i) for kind, i in PROJECT_QK]
SPLIT = ("k", "q", "ln")
N_SIDE, N_FIRST = len(SIDE), len(FIRST)
N_SPLIT = sum(s[1] in SPLIT for s in SIDE)
N_FIRST_SPLIT = sum(s[1] in SPLIT for s in FIRST)
ROWS4 = P // HD
STATS = LAST - 17


def at_slot(slot):
    for n, (at, kind, g, i) in enumerate(SIDE):
        if at == slot:
            yield n, sum(t[1] in SPLIT for t in SIDE[:n]), kind, g, i


def first_pieces():
    for n, (_, kind, g, i) in enumerate(FIRST):
        yield n, sum(t[1] in SPLIT for t in FIRST[:n]), kind, g, i


def beside_product(u):
    return u > 0 and u % PAIR == 0


def scores_in(u):
    if beside_product(u):
        return [u + LEAD, u + LEAD + 1]
    return [] if beside_product(u - 1) else [u + LEAD]


def number(kind, g, i):
    return next(n for n, s in enumerate(SIDE) if s[1:] == (kind, g, i))


def unit(u):
    g, s = divmod(u, UPG)
    return g, s // HPG, s % HPG


WEIGHTS = ("k", "q", "v")


def weight_load(kind, g):
    return len(WEIGHTS) * g + WEIGHTS.index(kind)


def adj_attention_block(nc, x, adj, wq, wk, wv, wo, y):
    with ExitStack() as ctx:
        def sb(name, shape, dt=F32):
            return ctx.enter_context(nc.sbuf_tensor(name, shape, dt))

        def sem(name):
            return ctx.enter_context(nc.semaphore(name))

        w_split = nc.dram_tensor("w_split", [3, G, P, 2 * DC * P], F32, kind="Internal").ap()
        k_split = nc.dram_tensor("k_split", [P, 2, N], F32, kind="Internal").ap()
        q_split = nc.dram_tensor("q_split", [P, 2, N], F32, kind="Internal").ap()
        o_split = nc.dram_tensor("o_split", [2, G, P, N], F32, kind="Internal").ap()

        ident = sb("ident", [P, P])
        hT = [sb("hT_hi", [P, DC, N], F32R), sb("hT_lo", [P, DC, N], F32R)]
        w_proj = sb("w_proj", [P, 2, 2, DC, P], F32R)
        w_out = sb("w_out", [P, 2, DC, D], F32R)
        qf = sb("qf", [P, 2, HALF], F32R)
        kf = sb("kf", [P, 2, HALF], F32R)
        vTh = sb("vTh", [P, HALF])
        q_stack = sb("q_stack", [P, HPG, N], F32R)
        k_stack = sb("k_stack", [P, 2, HPG, N], F32R)
        v_sb = sb("v_sb", [P, 2, MC, P])
        adj_sb = sb("adj_sb", [P, 2, N])
        neg_a = sb("neg_a", [P, 2, N])
        prob = sb("prob", [P, 2, N])
        probT = sb("probT", [P, HPG, MC, 2 * P])
        x_ln = sb("x_ln", [P, 2, D])
        x_res = sb("x_res", [P, 2, D])
        o_norm = sb("o_norm", [P, 2 * P])
        o_hl = sb("o_hl", [P, 2, 2 * P], F32R)
        o_in = sb("o_in", [P, 2, 2, G, P], F32R)
        tree = sb("tree", [P, 2, 512])
        leaf = sb("leaf", [P, PAIR, LEAF])
        neg_max = sb("neg_max", [P, 2, PAIR])
        neg_sum = sb("neg_sum", [P, PAIR])
        nonzero = sb("nonzero", [P, PAIR])
        rec_sum = sb("rec_sum", [P, PAIR])
        rec = sb("rec", [P, PAIR])
        row_sum = sb("row_sum", [P, 2, PAIR])
        rec_rep = sb("rec_rep", [P, 2, HPG, HD])
        row_stats = sb("row_stats", [P, 6 + 5 * NT])
        bn, mean_var = row_stats[:, 0:6], row_stats[:, 6:6 + 2 * NT].rearrange("p (t s) -> p t s", s=2)
        var_eps, rstd, newton = (row_stats[:, 6 + k * NT:6 + (k + 1) * NT] for k in (2, 3, 4))

        ps = ctx.enter_context(nc.psum_tensor("ps", [P, 8, HALF], F32))
        side = ps[:, 7, :]
        heads_out = ps[:, 6, 0:2 * P]

        s_apart = sem("waits_carried_apart")
        s_zero, s_ident = sem("ident_zeroed"), sem("ident_ready")
        s_wload = [sem(f"weights_loaded_{i}") for i in range(4)]
        s_wt, s_whi, s_wlo = sem("weights_turned"), sem("weights_hi"), sem("weights_lo")
        s_wst = sem("weights_stored")
        s_adj = [sem("adj_loaded_0"), sem("adj_loaded_1")]
        s_x = [sem("x_ln_loaded_0"), sem("x_ln_loaded_1")]
        s_xr = [sem("x_res_loaded_0"), sem("x_res_loaded_1")]
        s_wp = [sem("w_proj_loaded_0"), sem("w_proj_loaded_1")]
        s_oin = [sem("o_in_loaded_0"), sem("o_in_loaded_1")]
        s_kdr, s_qdr = sem("k_half_in_dram"), sem("q_half_in_dram")
        s_kst = sem("k_stacked")
        s_qst = [sem("q_stacked_0"), sem("q_stacked_1")]
        s_qk, s_max, s_exp = sem("scores_ready"), sem("max_ready"), sem("probs_ready")
        s_tree1, s_leaf = sem("scores_read_by_gpsimd"), sem("leaf_ready")
        s_tree2, s_leafsum = sem("tree_second_step"), sem("leaves_summed")
        s_turn = sem("probs_turned")
        s_copy = [sem("first_half_copied"), sem("second_half_copied")]
        s_rr, s_rstep = sem("rec_rep_ready"), sem("rec_step")
        s_pv1, s_pv = sem("first_chunks_read"), sem("heads_ready")
        s_norm, s_ohi, s_olo = sem("o_norm_ready"), sem("o_hi_ready"), sem("o_lo_ready")
        s_ost = sem("o_stored")
        s_piece, s_hi, s_evac = sem("piece_ready"), sem("piece_hi"), sem("piece_evacuated")
        s_bn, s_mv, s_ve, s_guess = sem("bn_ready"), sem("mean_var_ready"), sem("var_eps_ready"), sem("rstd_guessed")
        s_newton, s_xn = sem("newton_step"), sem("xn_ready")
        s_y = [sem("y_stored_0"), sem("y_stored_1")]

        w_dram = (wk, wq, wv, wo)
        w_stage = [hT[0][:].rearrange("p c (h e) -> p (c h) e", h=2), hT[1][:].rearrange("p c (h e) -> p (c h) e", h=2),
                   k_stack[:, 0].rearrange("p c (h e) -> p (c h) e", h=2), w_out[:].rearrange("p s c e -> p (s c) e")]
        w_raw = probT[:].rearrange("p h c n -> p (h c n)").rearrange("p (w o d) -> p w o d", w=4, o=DC)

        block = ctx.enter_context(nc.Block())


        def pieces_before(b):
            return 0 if b is None else N_FIRST + b * N_SIDE

        def splits_before(b):
            return 0 if b is None else N_FIRST_SPLIT + b * N_SPLIT

        def groups_before(b):
            return 0 if b is None else b * G

        def norms_before(b):
            return 0 if b is None else NT + b * NT

        def batches_normed(b):
            return 0 if b is None else b + 1

        def apart(eng):
            eng.sem_inc(s_apart, 1)

        @block.sync
        def _(sp):
            def load_weights(load):
                g, which = divmod(load, len(WEIGHTS))
                sp.dma_start(w_proj[:, load % 2].rearrange("p s c e -> p (s c e)").bitcast(F32),
                             w_split[which, g % G]).then_inc(s_wp[load % 2], 16)

            def store_half(kind, before, half):
                cols = slice(half * HALF, (half + 1) * HALF)
                if kind == "k":
                    sp.dma_start(k_split[:, :, cols], kf[:].bitcast(F32)).then_inc(s_kdr, 16)
                else:
                    sp.dma_start(q_split[:, :, cols], qf[:].bitcast(F32)).then_inc(s_qdr, 16)

            def stack_k(b, g):
                sp.wait_ge(s_kdr, 16 * 2 * (groups_before(b) + g + 1))
                apart(sp)
                for r in range(ROWS4):
                    sp.dma_start(k_stack[r * HD:(r + 1) * HD, g % 2].bitcast(F32),
                                 k_split[:, r % 2, :].rearrange("(h d) n -> d h n", d=HD)).then_inc(s_kst, 16)

            def stack_q(b, g, half):
                cols = slice(half * HALF, (half + 1) * HALF)
                if b is not None:
                    sp.wait_ge(s_qk, b * U + (g - 1) * UPG + (half + 1) * UPG // 2)
                    apart(sp)
                sp.wait_ge(s_qdr, 16 * (2 * (groups_before(b) + g) + half + 1))
                apart(sp)
                for r in range(ROWS4):
                    sp.dma_start(q_stack[r * HD:(r + 1) * HD, :, cols].bitcast(F32),
                                 q_split[:, r // 2, cols].rearrange("(h d) n -> d h n", d=HD)
                                 ).then_inc(s_qst[half], 16)

            def load_x(b, t):
                sp.dma_start(x_ln[:, t % 2, :], x[b, t * P:(t + 1) * P, :]).then_inc(s_x[t % 2], 16)

            def reload_x(b, xb, t):
                sp.wait_ge(s_bn, norms_before(b) + t + 1)
                apart(sp)
                load_x(xb, (t + 2) % NT)

            def load_adj(b, t):
                sp.dma_start(adj_sb[:, t % 2, :], adj[b, t * P:(t + 1) * P, :]).then_inc(s_adj[t % 2], 16)

            def store_heads(b, n):
                cols = slice((n % 4) * 2 * P, (n % 4 + 1) * 2 * P)
                sp.wait_ge(s_ohi, b * NP + n + 1)
                apart(sp)
                sp.wait_ge(s_olo, b * NP + n + 1)
                apart(sp)
                sp.dma_start(o_split[:, n // 4, :, cols].rearrange("s p n -> p s n"),
                             o_hl[:].bitcast(F32)).then_inc(s_ost, 16)

            def load_out_inputs(b, t):
                rows = slice(t * P, (t + 1) * P)
                if t >= 2:
                    sp.wait_ge(s_y[t % 2], 16 * (b * (NT // 2) + t // 2))
                    apart(sp)
                sp.dma_start(x_res[:, t % 2, :], x[b, rows, :]).then_inc(s_xr[t % 2], 16)
                sp.wait_ge(s_ost, 16 * (b * NP + (G - 1) * 4 + t // 2 + 1))
                apart(sp)
                for part in (HI, LO):
                    sp.dma_start(o_in[:, t % 2, part].bitcast(F32), o_split[part, :, :, rows].rearrange("g p n -> p g n")
                                 ).then_inc(s_oin[t % 2], 16)

            def after_piece(b, xb, n, kind, g, i):
                done = pieces_before(b) + n + 1
                if kind == "ln" and i + 2 < NT:
                    sp.wait_ge(s_piece, done)
                    apart(sp)
                    load_x(xb, i + 2)
                if kind in ("k", "q"):
                    before = groups_before(b) + g
                    if b is not None:
                        sp.wait_ge(s_kst if kind == "k" else s_qst[i], 16 * ROWS4 * before)
                        apart(sp)
                    sp.wait_ge(s_evac, done)
                    apart(sp)
                    store_half(kind, before, i)
                if kind in WEIGHTS and i == 1:
                    sp.wait_ge(s_piece, done)
                    apart(sp)
                    load_weights(weight_load(kind, g) + 2)
                if kind == "out":
                    sp.wait_ge(s_evac, done)
                    apart(sp)
                    sp.dma_start(y[b, i * P:(i + 1) * P, :], x_res[:, i % 2, :]).then_inc(s_y[i % 2], 16)

            load_x(0, 0)
            load_x(0, 1)
            for i, w in enumerate(w_dram):
                sp.dma_start(w_raw[:, i], w.rearrange("(o p) d -> p o d", p=P)).then_inc(s_wload[i], 16)
                for t in (2 * i, 2 * i + 1):
                    reload_x(None, 0, t)
            load_adj(0, 0)
            for i in range(len(WEIGHTS)):
                sp.wait_ge(s_whi, DC * (i + 1))
                sp.wait_ge(s_wlo, DC * (i + 1))
                for g in range(G):
                    sp.dma_start(w_split[i, g].rearrange("p (s e) -> p s e", e=P),
                                 w_stage[i][:, :, g * P:(g + 1) * P].bitcast(F32)).then_inc(s_wst, 16)
            sp.wait_ge(s_wst, 16 * len(WEIGHTS) * G)
            load_weights(0)
            load_weights(1)
            for n, _, kind, g, i in first_pieces():
                after_piece(None, 0, n, kind, g, i)
            stack_k(None, 0)
            for half in range(2):
                stack_q(None, 0, half)

            with sp.Fori(0, B) as b:
                nb = (b + 1) % B
                for u in range(U):
                    g, s = divmod(u, UPG)
                    if s % HPG == 0:
                        t = u // HPG + 1
                        if u:
                            sp.wait_ge(s_max, b * U + u)
                            apart(sp)
                        load_adj(b if t < NT * G else nb, t % NT)
                    if u > 0:
                        for n, _, kind, pg, i in at_slot(u - 1):
                            after_piece(b, nb, n, kind, pg, i)
                    if s == (18 if g + 1 < G else 25):
                        stack_q(b, g + 1, 0)
                    if s == (21 if g + 1 < G else 26):
                        stack_k(b, g + 1)
                    if s == UPG - 1:
                        stack_q(b, g + 1, 1)
                    if u >= PAIR + 3 and (u - 3) % PAIR == 0:
                        store_heads(b, (u - 3) // PAIR - 1)
                    if u in (STATS - 3, STATS - 2):
                        load_x(nb, u - STATS + 3)
                    if STATS < u <= STATS + 2 * NT and (u - STATS) % 2:
                        reload_x(b, nb, (u - STATS) // 2)
                    for t, at in ((0, 13), (1, 13), (2, 21), (3, 21), (4, 29), (5, 29)):
                        if u == LAST + at:
                            load_out_inputs(b, t)
                for n, _, kind, pg, i in at_slot(U - 1):
                    after_piece(b, nb, n, kind, pg, i)
                store_heads(b, NP - 1)
                load_out_inputs(b, NT - 2)
                for n, _, kind, pg, i in at_slot(U):
                    after_piece(b, nb, n, kind, pg, i)
                    if kind == "out" and i == NT - 3:
                        load_out_inputs(b, NT - 1)
                for i in range(2):
                    sp.wait_ge(s_y[i], 16 * (b * (NT // 2) + NT // 2))
                    apart(sp)

            for i in range(2):
                sp.wait_ge(s_y[i], 16 * B * NT // 2)
                apart(sp)
                sp.wait_ge(s_wp[i], 16 * (B * G * len(WEIGHTS) // 2 + 2))
                apart(sp)
            sp.wait_ge(s_adj[0], 16 * (B * G * NT // 2 + 1))
            apart(sp)

        @block.gpsimd
        def _(pool):
            def rstd_of(k):
                pool.wait_ge(s_guess, k + 1)
                for step in range(NEWTON):
                    done = (k * NEWTON + step) * 4
                    pool.tensor_tensor(newton, rstd, rstd, ALU.mult).then_inc(s_newton, 1)
                    pool.wait_ge(s_newton, done + 1)
                    pool.tensor_tensor(newton, newton, var_eps, ALU.mult).then_inc(s_newton, 1)
                    pool.wait_ge(s_newton, done + 2)
                    apart(pool)
                    pool.tensor_scalar(newton, newton, -0.5, 1.5, ALU.mult, ALU.add).then_inc(s_newton, 1)
                    pool.wait_ge(s_newton, done + 3)
                    pool.tensor_tensor(rstd, rstd, newton, ALU.mult).then_inc(s_newton, 1)
                    if step + 1 < NEWTON:
                        pool.wait_ge(s_newton, done + 4)

            def halve_first(b, u):
                pool.wait_ge(s_max, b * U + u + 1)
                if u >= 2:
                    pool.wait_ge(s_leaf, b * U + u - 1)
                pool.tensor_tensor(tree[:, u % 2, :], neg_a[:, u % 2, 0:512], neg_a[:, u % 2, 512:1024],
                                   ALU.add).then_inc(s_tree1, 1)

            def halve_second(b, u):
                pool.wait_ge(s_tree1, b * U + u + 1)
                pool.tensor_tensor(tree[:, u % 2, 0:256], tree[:, u % 2, 0:256], tree[:, u % 2, 256:512],
                                   ALU.add).then_inc(s_tree2, 1)

            def halve_last(b, u):
                pool.wait_ge(s_tree2, b * U + u + 1)
                if u % PAIR == 0:
                    pool.wait_ge(s_leafsum, b * NP + u // PAIR + 1)
                pool.tensor_tensor(leaf[:, u % PAIR, :], tree[:, u % 2, 0:128], tree[:, u % 2, 128:256],
                                   ALU.add).then_inc(s_leaf, 1)

            pool.sem_inc(s_leafsum, 1)
            pool.memset(ident[:], 0.0).then_inc(s_zero, 1)
            pool.wait_ge(s_zero, 1)
            pool.affine_select(out=ident[:], in_=ident[:], compare_op=ALU.not_equal, fill=1.0, base=0,
                               pattern=[[-1, P]], channel_multiplier=1).then_inc(s_ident, 1)
            rstd_of(0)

            with pool.Fori(0, B) as b:
                for u in range(U):
                    halve_first(b, u)
                    if u:
                        halve_last(b, u - 1)
                    halve_second(b, u)
                    if u == STATS + 2 * NT:
                        rstd_of(b + 1)
                halve_last(b, U - 1)

        @block.tensor
        def _(pe):
            def scores(b, u):
                g, t, h = unit(u)
                if u >= 2:
                    pe.wait_ge(s_max, b * U + u - 1)
                if u % UPG == 0:
                    pe.wait_ge(s_kst, 16 * ROWS4 * (b * G + g + 1))
                    pe.wait_ge(s_qst[0], 16 * ROWS4 * (b * G + g + 1))
                if u % UPG == UPG // 2:
                    pe.wait_ge(s_qst[1], 16 * ROWS4 * (b * G + g + 1))
                for half in range(2):
                    mm = pe.matmul(ps[:, 2 * (u % 2) + half, :], q_stack[:, h, t * P:(t + 1) * P],
                                   k_stack[:, g % 2, h, half * HALF:(half + 1) * HALF], start=True, stop=True)
                mm.then_inc(s_qk, 1)

            def turn_probs(b, u):
                pe.wait_ge(s_exp, b * U + u + 1)
                for half in range(2):
                    if u:
                        pe.wait_ge(s_copy[half], b * U + u)
                    for c in range(4):
                        mm = pe.transpose(ps[:, 4 + half, c * P:(c + 1) * P],
                                          prob[:, u % 2, (4 * half + c) * P:(4 * half + c + 1) * P], ident[:])
                    mm.then_inc(s_turn, 1)

            def times_v(b, n):
                g = n // 4
                if n:
                    pe.wait_ge(s_norm, b * NP + n)
                pe.wait_ge(s_copy[0], b * U + PAIR * (n + 1))
                pe.wait_ge(s_copy[1], b * U + PAIR * (n + 1))
                pe.wait_ge(s_evac, pieces_before(b) + number("vt", g, 1) + 1)
                for c in range(MC):
                    for h in range(HPG):
                        mm = pe.matmul(ps[h * HD:(h + 1) * HD, 6, 0:2 * P], v_sb[:, g % 2, c, h * HD:(h + 1) * HD],
                                       probT[:, h, c, :], start=(c == 0), stop=(c == MC - 1))
                    if c == MC // 2 - 1:
                        mm.then_inc(s_pv1, 1)
                mm.then_inc(s_pv, 1)

            def piece(b, n, kind, g, i):
                if n or b is not None:
                    pe.wait_ge(s_evac, pieces_before(b) + n)
                if kind in WEIGHTS:
                    load = weight_load(kind, g)
                    if i == 0:
                        loads = 0 if b is None else b * (G * len(WEIGHTS) // 2)
                        pe.wait_ge(s_wp[load % 2], 16 * (loads + load // 2 + 1))
                    for k, (c, (pw, ph)) in enumerate((c, p) for c in range(DC) for p in PRODUCTS):
                        mm = pe.matmul(side, w_proj[:, load % 2, pw, c, :], hT[ph][:, c, i * HALF:(i + 1) * HALF],
                                       start=(k == 0), stop=(k == DC * len(PRODUCTS) - 1))
                elif kind == "vt":
                    for c in range(4):
                        mm = pe.transpose(side[:, c * P:(c + 1) * P], vTh[:, c * P:(c + 1) * P], ident[:])
                elif kind == "ln":
                    pe.wait_ge(s_xn, norms_before(b) + i + 1)
                    for c in range(DC):
                        mm = pe.transpose(side[:, c * P:(c + 1) * P], x_ln[:, i % 2, c * P:(c + 1) * P], ident[:])
                elif kind == "r":
                    pe.wait_ge(s_rr, b * NP + i + 1)
                    for j in range(2):
                        mm = pe.transpose(side[:, j * P:(j + 1) * P],
                                          rec_rep[:, j].rearrange("p h d -> p (h d)"), ident[:])
                else:
                    pe.wait_ge(s_oin[i % 2], 32 * (b * (NT // 2) + i // 2 + 1))
                    for k, (c, (po, pw)) in enumerate((c, p) for c in range(G) for p in PRODUCTS):
                        mm = pe.matmul(side, o_in[:, i % 2, po, c, :], w_out[:, pw, c, :],
                                       start=(k == 0), stop=(k == G * len(PRODUCTS) - 1))
                mm.then_inc(s_piece, 1)

            pe.wait_ge(s_ident, 1)
            for k in range(4 * DC):
                w, ic = divmod(k, DC)
                if ic == 0:
                    pe.wait_ge(s_wload[w], 16)
                if k >= 4:
                    pe.wait_ge(s_wlo, k - 3)
                for oc in range(DC):
                    mm = pe.transpose(ps[:, k % 4, oc * P:(oc + 1) * P],
                                      w_raw[:, w, oc, ic * P:(ic + 1) * P], ident[:])
                mm.then_inc(s_wt, 1)
            pe.wait_ge(s_wlo, 4 * DC)
            for n, _, kind, g, i in first_pieces():
                piece(None, n, kind, g, i)

            for u in range(LEAD):
                scores(0, u)
            with pe.Fori(0, B) as b:
                for u in range(U):
                    for ahead in scores_in(u)[:1]:
                        scores(b, ahead)
                    turn_probs(b, u)
                    for ahead in scores_in(u)[1:]:
                        scores(b, ahead)
                    if beside_product(u):
                        times_v(b, u // PAIR - 1)
                    for n, _, kind, g, i in at_slot(u):
                        piece(b, n, kind, g, i)
                times_v(b, NP - 1)
                for n, _, kind, g, i in at_slot(U):
                    piece(b, n, kind, g, i)

        @block.scalar
        def _(act):
            def probs(b, u):
                n = u // PAIR
                act.wait_ge(s_max, b * U + u + 1)
                if u >= 2:
                    act.wait_ge(s_turn, (b * U + u - 1) * 2)
                act.activation(prob[:, u % 2, :], neg_a[:, u % 2, :], ACT.Exp,
                               bias=neg_max[:, n % 2, u % PAIR:u % PAIR + 1], scale=-1.0,
                               accum_out=row_sum[:, n % 2, u % PAIR:u % PAIR + 1]).then_inc(s_exp, 1)

            def copy_turned(b, u):
                _, t, h = unit(u)
                act.wait_ge(s_turn, (b * U + u) * 2 + 1)
                if u >= PAIR:
                    act.wait_ge(s_pv1, b * NP + u // PAIR)
                act.copy(probT[:, h, 0:4, (t % 2) * P:(t % 2 + 1) * P],
                         ps[:, 4, :].rearrange("p (c n) -> p c n", n=P)).then_inc(s_copy[0], 1)

            def split_hi(b, n, m, kind, g, i):
                if kind not in SPLIT:
                    return
                act.wait_ge(s_piece, pieces_before(b) + n + 1)
                if kind == "k":
                    if b is not None or i:
                        act.wait_ge(s_kdr, 16 * ((groups_before(b) + g) * 2 + i))
                    act.copy(kf[:, HI, :], side).then_inc(s_hi, 1)
                elif kind == "q":
                    if b is not None or i:
                        act.wait_ge(s_qdr, 16 * ((groups_before(b) + g) * 2 + i))
                    act.mul(qf[:, HI, :], side, QSCALE).then_inc(s_hi, 1)
                else:
                    act.activation(hT[HI][:, :, i * P:(i + 1) * P], side.rearrange("p (c n) -> p c n", n=P),
                                   ACT.Relu).then_inc(s_hi, 1)

            def heads_hi(b, n):
                act.wait_ge(s_norm, b * NP + n + 1)
                if n:
                    act.wait_ge(s_ost, 16 * (b * NP + n))
                act.copy(o_hl[:, HI, :], o_norm[:]).then_inc(s_ohi, 1)

            for k in range(4 * DC):
                w, ic = divmod(k, DC)
                act.wait_ge(s_wt, k + 1)
                act.copy(w_stage[w][:, HI * DC + ic, :], ps[:, k % 4, :]).then_inc(s_whi, 1)
            act.wait_ge(s_wst, 16 * len(WEIGHTS) * G)
            for n, m, kind, g, i in first_pieces():
                split_hi(None, n, m, kind, g, i)

            probs(0, 0)
            with act.Fori(0, B) as b:
                for u in range(U):
                    if not beside_product(u - 1):
                        probs(b, u + 1)
                    if u:
                        for n, m, kind, g, i in at_slot(u - 1):
                            split_hi(b, n, m, kind, g, i)
                    if beside_product(u):
                        probs(b, u + 2)
                    copy_turned(b, u)
                    if u > PAIR and u % PAIR == 1:
                        heads_hi(b, u // PAIR - 1)
                heads_hi(b, NP - 1)
                for n, m, kind, g, i in at_slot(U):
                    split_hi(b, n, m, kind, g, i)

        @block.vector
        def _(dve):
            def bias_and_max(b, u):
                _, t, _ = unit(u)
                n = u // PAIR
                tile = u // HPG
                dve.wait_ge(s_qk, b * U + u + 1)
                if u % HPG == 0:
                    dve.wait_ge(s_adj[tile % 2], 16 * (b * (G * NT // 2) + tile // 2 + 1))
                if u >= 2:
                    dve.wait_ge(s_exp, b * U + u - 1)
                    dve.wait_ge(s_tree1, b * U + u - 1)
                apart(dve)
                dve.tensor_tensor_reduce(
                    neg_a[:, u % 2, :], ps[:, 2 * (u % 2):2 * (u % 2) + 2, :].rearrange("p h m -> p (h m)"),
                    adj_sb[:, tile % 2, :], -2.0, 3.0e38, ALU.add, ALU.min,
                    neg_max[:, n % 2, u % PAIR:u % PAIR + 1]).then_inc(s_max, 1)

            def copy_turned(b, u):
                _, t, h = unit(u)
                dve.wait_ge(s_turn, (b * U + u) * 2 + 2)
                if u >= PAIR:
                    dve.wait_ge(s_pv, b * NP + u // PAIR)
                dve.tensor_copy(probT[:, h, 4:8, (t % 2) * P:(t % 2 + 1) * P],
                                ps[:, 5, :].rearrange("p (c n) -> p c n", n=P)).then_inc(s_copy[1], 1)

            def reciprocals(b, n):
                steps = (b * NP + n) * 4
                dve.wait_ge(s_leaf, b * U + PAIR * (n + 1))
                dve.wait_ge(s_exp, b * U + PAIR * (n + 1))
                dve.tensor_reduce(neg_sum[:], leaf[:], AX.X, ALU.add).then_inc(s_leafsum, 1)
                dve.reciprocal(rec_sum[:], row_sum[:, n % 2]).then_inc(s_rstep, 1)
                dve.tensor_scalar(nonzero[:], neg_max[:, n % 2], 0.0, None, ALU.not_equal).then_inc(s_rstep, 1)
                dve.wait_ge(s_leafsum, b * NP + n + 2)
                dve.wait_ge(s_rstep, steps + 2)
                dve.scalar_tensor_tensor(nonzero[:], neg_sum[:], 0.0, nonzero[:], ALU.not_equal, ALU.max
                                         ).then_inc(s_rstep, 1)
                dve.wait_ge(s_rstep, steps + 3)
                dve.tensor_tensor(rec[:], nonzero[:], rec_sum[:], ALU.mult).then_inc(s_rstep, 1)
                dve.wait_ge(s_rstep, steps + 4)
                dve.tensor_copy(rec_rep[:].rearrange("p j h d -> p (j h) d"),
                                rec[:].unsqueeze(2).to_broadcast([P, PAIR, HD])).then_inc(s_rr, 1)

            def tile_stats(b, t):
                k = norms_before(b) + t
                dve.wait_ge(s_x[t % 2], 16 * (NT * batches_normed(b) + t // 2 + 1))
                if b is not None or t:
                    dve.wait_ge(s_mv, k)
                dve.bn_stats(bn, x_ln[:, t % 2, :]).then_inc(s_bn, 1)
                dve.wait_ge(s_bn, k + 1)
                apart(dve)
                dve.bn_aggr(mean_var[:, t, :], bn).then_inc(s_mv, 1)

            def rstd_guess(b):
                dve.wait_ge(s_mv, norms_before(b) + NT)
                dve.tensor_scalar(var_eps, mean_var[:, :, 1], EPS, None, ALU.add).then_inc(s_ve, 1)
                dve.wait_ge(s_ve, batches_normed(b) + 1)
                dve.tensor_scalar(rstd.bitcast(I32), var_eps.bitcast(I32), -0.5, RSQRT_BITS,
                                  ALU.mult, ALU.add).then_inc(s_guess, 1)

            def tile_norm(b, t):
                dve.wait_ge(s_x[t % 2], 16 * (NT * batches_normed(b) + NT // 2 + t // 2 + 1))
                dve.wait_ge(s_newton, (batches_normed(b) + 1) * NEWTON * 4)
                dve.tensor_scalar(x_ln[:, t % 2, :], x_ln[:, t % 2, :], mean_var[:, t, 0:1], rstd[:, t:t + 1],
                                  ALU.subtract, ALU.mult).then_inc(s_xn, 1)

            def evacuate(b, n, m, kind, g, i):
                dve.wait_ge(s_piece, pieces_before(b) + n + 1)
                if kind in SPLIT:
                    dve.wait_ge(s_hi, splits_before(b) + m + 1)
                side_c = side.rearrange("p (c n) -> p c n", n=P)
                if kind == "k":
                    op = dve.scalar_tensor_tensor(kf[:, LO, :], side, 1.0, kf[:, HI, :].bitcast(F32),
                                                  ALU.mult, ALU.subtract)
                elif kind == "q":
                    op = dve.scalar_tensor_tensor(qf[:, LO, :], side, QSCALE, qf[:, HI, :].bitcast(F32),
                                                  ALU.mult, ALU.subtract)
                elif kind == "ln":
                    rows = slice(i * P, (i + 1) * P)
                    op = dve.scalar_tensor_tensor(hT[LO][:, :, rows], side_c, 0.0, hT[HI][:, :, rows].bitcast(F32),
                                                  ALU.max, ALU.subtract)
                elif kind == "v":
                    op = dve.tensor_copy(vTh[:], side)
                elif kind == "vt":
                    op = dve.tensor_copy(v_sb[:, g % 2, 4 * i:4 * i + 4, :], side_c)
                elif kind == "r":
                    op = dve.tensor_copy(o_norm[:], side[:, 0:2 * P])
                else:
                    dve.wait_ge(s_xr[i % 2], 16 * (b * (NT // 2) + i // 2 + 1))
                    op = dve.tensor_tensor(x_res[:, i % 2, :], side, x_res[:, i % 2, :], ALU.add)
                op.then_inc(s_evac, 1)
                if kind == "r":
                    dve.wait_ge(s_pv, b * NP + i + 1)
                    dve.wait_ge(s_evac, pieces_before(b) + n + 1)
                    dve.tensor_tensor(o_norm[:], heads_out, o_norm[:], ALU.mult).then_inc(s_norm, 1)

            def heads_lo(b, n):
                dve.wait_ge(s_ohi, b * NP + n + 1)
                dve.tensor_tensor(o_hl[:, LO, :], o_norm[:], o_hl[:, HI, :].bitcast(F32), ALU.subtract
                                  ).then_inc(s_olo, 1)

            for t in range(NT):
                tile_stats(None, t)
            rstd_guess(None)
            for k in range(4 * DC):
                w, ic = divmod(k, DC)
                dve.wait_ge(s_whi, k + 1)
                dve.scalar_tensor_tensor(w_stage[w][:, LO * DC + ic, :], ps[:, k % 4, :], 1.0,
                                         w_stage[w][:, HI * DC + ic, :].bitcast(F32),
                                         ALU.mult, ALU.subtract).then_inc(s_wlo, 1)
            dve.wait_ge(s_wst, 16 * len(WEIGHTS) * G)
            for n, m, kind, g, i in first_pieces():
                if kind == "ln":
                    tile_norm(None, i)
                evacuate(None, n, m, kind, g, i)

            for u in range(LEAD):
                bias_and_max(0, u)
            with dve.Fori(0, B) as b:
                for u in range(U):
                    for ahead in scores_in(u)[:1]:
                        bias_and_max(b, ahead)
                    if u % PAIR == 2 and u > PAIR:
                        heads_lo(b, u // PAIR - 1)
                    if u:
                        for n, m, kind, g, i in at_slot(u - 1):
                            evacuate(b, n, m, kind, g, i)
                    if u > LAST and (u - LAST) % 2 and (u - LAST) // 2 < NT:
                        tile_norm(b, (u - LAST) // 2)
                    if beside_product(u):
                        reciprocals(b, u // PAIR - 1)
                    if STATS <= u < STATS + 2 * NT and (u - STATS) % 2 == 0:
                        tile_stats(b, (u - STATS) // 2)
                    if u == STATS + 2 * NT - 1:
                        rstd_guess(b)
                    for ahead in scores_in(u)[1:]:
                        bias_and_max(b, ahead)
                    copy_turned(b, u)
                reciprocals(b, NP - 1)
                for n, m, kind, g, i in at_slot(U - 1):
                    evacuate(b, n, m, kind, g, i)
                for n, m, kind, g, i in at_slot(U):
                    evacuate(b, n, m, kind, g, i)
                    if kind == "r":
                        heads_lo(b, NP - 1)


_INS = ["x", "adj", "L0_gnn_Wq", "L0_gnn_Wk", "L0_gnn_Wv", "L0_gnn_Wo"]


def kernel(**inputs):
    import concourse.bacc as bacc
    from concourse.bass_utils import run_bass_kernel_spmd

    nc = bacc.Bacc("TRN2", target_bir_lowering=False, num_devices=1)
    arrays, args = {}, []
    for name in _INS:
        a = np.ascontiguousarray(inputs[name])
        arrays[f"in_{name}"] = a
        args.append(nc.dram_tensor(f"in_{name}", a.shape, mybir.dt.from_np(a.dtype), kind="ExternalInput").ap())
    out = nc.dram_tensor("out_y", (B, N, D), F32, kind="ExternalOutput").ap()
    adj_attention_block(nc, *args, out)
    r = run_bass_kernel_spmd(nc, [arrays], core_ids=[0])
    return r.results[0]["out_y"]
```

```python
from contextlib import ExitStack

import numpy as np

import concourse.bass as bass
from concourse import mybir

ALU = mybir.AluOpType
ACT = mybir.ActivationFunctionType
AX = mybir.AxisListType
F32 = mybir.dt.float32
F32R = mybir.dt.float32r
I32 = mybir.dt.int32

P = 128
B, N, D, HEADS = 8, 1024, 512, 16
HD = D // HEADS
HPG = P // HD
G = HEADS // HPG
NT = N // P
MC = N // P
DC = D // P
HALF = N // 2
UPG = NT * HPG
U = G * UPG
PAIR = 2 * HPG
NP = U // PAIR
LEAF = 128
EPS = 1e-5
NEWTON = 3
RSQRT_BITS = float(0x5F3759DF)
QSCALE = float(D) ** -0.5 / 2.0
HI, LO = 0, 1
PRODUCTS = ((HI, HI), (HI, LO), (LO, HI))

LAST = (G - 1) * UPG
BEGIN = 3 * PAIR
QK_V = (("k", 0), ("q", 0), ("k", 1), ("q", 1), ("v", 0), ("vt", 0), ("v", 1), ("vt", 1))


def side(group, kinds, slots, base=0):
    return [(tuple(base + s for s in at), kind, group, i) for (kind, i), at in zip(kinds, slots)]


def q_k_of_second(base, group):
    return side(group, QK_V[:4], ((11, 12), (15, 17), (20, 21), (22, 23)), base)


SIDE = side(1, QK_V[4:], ((25, 26, 27), (28,), (29, 30, 31), (33,)))
SIDE += side(2, QK_V, ((35, 36, 37), (38, 39, 41), (42, 43, 44), (45, 46, 47), (50, 51, 52), (54,), (55, 57, 58), (60,)))
SIDE += side(3, QK_V, ((61, 62, 63), (65, 66, 67), (68, 69, 70), (71, 73, 74), (75, 76, 77), (79,), (81, 82, 83), (85,)))
SIDE += side(G, [("ln", t) for t in range(NT)], [(87 + 2 * t,) for t in range(NT)])
SIDE += side(G, QK_V, ((102, 103, 105), (106, 107, 108), (109, 110, 111), (113, 114, 115), (126, 127), (129,),
                       (130, 131), (133,)))
SIDE += side(G, [("out", t) for t in range(NT)],
             ((116, 117), (118, 119), (122, 123), (124, 125), (134, 135), (137, 138), (141, 142), (146, 147)))
SIDE += q_k_of_second(U, G + 1)
SIDE.sort()
STACK_K, STACK_Q = (26, 21, 21, 26), (23, 18, 18, 22)
OUT_LOADS = (13, 13, 22, 24, 28, 30, 41, 43)
FIRST = [((), "ln", 0, t) for t in range(NT)] + [((), kind, 0, i) for kind, i in QK_V[:4]]
FIRST += side(0, QK_V[4:], ((1, 2), (3,), (4, 5), (6,))) + q_k_of_second(0, 1)
END = [p for p in SIDE if p[1] == "out" or p[2] < G]
assert all(a[0][-1] < b[0][0] for a, b in zip(SIDE, SIDE[1:]))
LEAD = 2
SPLIT = ("k", "q", "ln")
ROWS4 = P // HD
STATS, STATS_STEP = LAST - 45, 4
STATS_END = STATS + STATS_STEP * NT


def n_split(pieces):
    return sum(kind in SPLIT for _, kind, _, _ in pieces)


def finished_at(pieces, slot):
    for n, (slots, kind, g, i) in enumerate(pieces):
        if slots and slots[-1] == slot:
            yield n, n_split(pieces[:n]), kind, g, i


def parts_at(pieces, slot):
    for n, (slots, kind, g, i) in enumerate(pieces):
        if slot in slots:
            yield n, slots.index(slot), len(slots), kind, g, i


def before_units():
    for n, (slots, kind, g, i) in enumerate(FIRST):
        if not slots:
            yield n, n_split(FIRST[:n]), kind, g, i


def before(b, pieces):
    return 0 if pieces is FIRST else len(FIRST) + b * len(SIDE)


def splits_before(b, pieces):
    return 0 if pieces is FIRST else n_split(FIRST) + b * n_split(SIDE)


def beside_product(u):
    return u > 0 and u % PAIR == 0


def units_of(pieces, units):
    return [u for u in units if u < U or pieces is not END]


def scores_in(u, pieces):
    if beside_product(u):
        ahead = [u + LEAD], [u + LEAD + 1]
    else:
        ahead = [] if beside_product(u - 1) else [u + LEAD], []
    return [units_of(pieces, units) for units in ahead]


def product_at(slot, u, pieces):
    n = (u - slot) // PAIR - 1
    return [n] if (u - slot) % PAIR == 0 and n >= 0 and (n < NP or pieces is not END) else []


def number(pieces, kind, g, i):
    return next(n for n, p in enumerate(pieces) if p[1:] == (kind, g, i))


def unit(u):
    g, s = divmod(u, UPG)
    return g, s // HPG, s % HPG


WEIGHTS = ("k", "q", "v")


def weight_load(kind, g):
    return len(WEIGHTS) * g + WEIGHTS.index(kind)


def adj_attention_block(nc, x, adj, wq, wk, wv, wo, y):
    with ExitStack() as ctx:
        def sb(name, shape, dt=F32):
            return ctx.enter_context(nc.sbuf_tensor(name, shape, dt))

        def sem(name):
            return ctx.enter_context(nc.semaphore(name))

        w_split = nc.dram_tensor("w_split", [3, G, P, 2 * DC * P], F32, kind="Internal").ap()
        k_split = nc.dram_tensor("k_split", [P, 2, N], F32, kind="Internal").ap()
        q_split = nc.dram_tensor("q_split", [P, 2, N], F32, kind="Internal").ap()
        o_split = nc.dram_tensor("o_split", [2, G, P, N], F32, kind="Internal").ap()

        ident = sb("ident", [P, P])
        hT = [sb("hT_hi", [P, DC, N], F32R), sb("hT_lo", [P, DC, N], F32R)]
        w_proj = sb("w_proj", [P, 2, 2, DC, P], F32R)
        w_out = sb("w_out", [P, 2, DC, D], F32R)
        qf = sb("qf", [P, 2, HALF], F32R)
        kf = sb("kf", [P, 2, HALF], F32R)
        vTh = sb("vTh", [P, HALF])
        q_stack = sb("q_stack", [P, HPG, N], F32R)
        k_stack = sb("k_stack", [P, 2, HPG, N], F32R)
        v_sb = sb("v_sb", [P, 2, MC, P])
        adj_sb = sb("adj_sb", [P, 2, N])
        neg_a = sb("neg_a", [P, 2, N])
        prob = sb("prob", [P, 2, N])
        probT = sb("probT", [P, HPG, MC, 2 * P])
        x_ln = sb("x_ln", [P, 2, D])
        x_res = sb("x_res", [P, 2, D])
        o_norm = sb("o_norm", [P, 2 * P])
        o_hl = sb("o_hl", [P, 2, 2 * P], F32R)
        o_in = sb("o_in", [P, 2, 2, G, P], F32R)
        tree = sb("tree", [P, 2, 512])
        leaf = sb("leaf", [P, PAIR, LEAF])
        neg_max = sb("neg_max", [P, 2, PAIR])
        neg_sum = sb("neg_sum", [P, PAIR])
        nonzero = sb("nonzero", [P, PAIR])
        rec_sum = sb("rec_sum", [P, PAIR])
        rec = sb("rec", [P, PAIR])
        row_sum = sb("row_sum", [P, 2, PAIR])
        rec_rep = sb("rec_rep", [P, 2, HPG, HD])
        row_stats = sb("row_stats", [P, 6 + 6 * NT])
        bn, mean_var = row_stats[:, 0:6], row_stats[:, 6:6 + 2 * NT].rearrange("p (t s) -> p t s", s=2)
        var_eps, rstd, newton, shift = (row_stats[:, 6 + k * NT:6 + (k + 1) * NT] for k in (2, 3, 4, 5))

        ps = ctx.enter_context(nc.psum_tensor("ps", [P, 8, HALF], F32))
        side_bank = ps[:, 7, :]
        heads_out, rec_out = ps[:, 6, 0:2 * P], ps[:, 6, 2 * P:4 * P]

        s_apart = sem("waits_carried_apart")
        s_zero, s_ident = sem("ident_zeroed"), sem("ident_ready")
        s_wload = [sem(f"weights_loaded_{i}") for i in range(4)]
        s_wt, s_whi, s_wlo = sem("weights_turned"), sem("weights_hi"), sem("weights_lo")
        s_wst = sem("weights_stored")
        s_adj = [sem("adj_loaded_0"), sem("adj_loaded_1")]
        s_x = [sem("x_ln_loaded_0"), sem("x_ln_loaded_1")]
        s_xr = [sem("x_res_loaded_0"), sem("x_res_loaded_1")]
        s_wp = [sem("w_proj_loaded_0"), sem("w_proj_loaded_1")]
        s_oin = [sem("o_in_loaded_0"), sem("o_in_loaded_1")]
        s_kdr, s_qdr = sem("k_half_in_dram"), sem("q_half_in_dram")
        s_kst = sem("k_stacked")
        s_qst = [sem("q_stacked_0"), sem("q_stacked_1")]
        s_qk, s_max, s_exp = sem("scores_ready"), sem("max_ready"), sem("probs_ready")
        s_tree1, s_leaf = sem("scores_read_by_gpsimd"), sem("leaf_ready")
        s_tree2, s_leafsum = sem("tree_second_step"), sem("leaves_summed")
        s_turn = sem("probs_turned")
        s_copy = [sem("first_half_copied"), sem("second_half_copied")]
        s_rr, s_rstep = sem("rec_rep_ready"), sem("rec_step")
        s_rt, s_rc = sem("rec_turned"), sem("rec_copied")
        s_pv1, s_pv = sem("first_chunks_read"), sem("heads_ready")
        s_norm, s_ohi, s_olo = sem("o_norm_ready"), sem("o_hi_ready"), sem("o_lo_ready")
        s_ost = sem("o_stored")
        s_piece, s_hi, s_evac = sem("piece_ready"), sem("piece_hi"), sem("piece_evacuated")
        s_bn, s_mv, s_ve, s_guess = sem("bn_ready"), sem("mean_var_ready"), sem("var_eps_ready"), sem("rstd_guessed")
        s_newton, s_xn = sem("newton_step"), sem("xn_ready")
        s_shifting, s_shift = sem("mean_times_rstd"), sem("shift_ready")
        s_y = [sem("y_stored_0"), sem("y_stored_1")]

        w_dram = (wk, wq, wv, wo)
        w_stage = [s.rearrange("p c (h e) -> p (c h) e", h=2) for s in (k_stack[:, 0], k_stack[:, 1], q_stack[:])]
        w_stage.append(w_out[:].rearrange("p s c e -> p (s c) e"))
        w_raw = probT[:].rearrange("p h c n -> p (h c n)").rearrange("p (w o d) -> p w o d", w=4, o=DC)

        block = ctx.enter_context(nc.Block())

        def apart(eng):
            eng.sem_inc(s_apart, 1)

        @block.sync
        def _(sp):
            def load_weights(load):
                g, which = divmod(load, len(WEIGHTS))
                sp.dma_start(w_proj[:, load % 2].rearrange("p s c e -> p (s c e)").bitcast(F32),
                             w_split[which, g % G]).then_inc(s_wp[load % 2], 16)

            def store_split_weights(i):
                sp.wait_ge(s_whi, DC * (i + 1))
                sp.wait_ge(s_wlo, DC * (i + 1))
                for g in range(G):
                    sp.dma_start(w_split[i, g].rearrange("p (s e) -> p s e", e=P),
                                 w_stage[i][:, :, g * P:(g + 1) * P].bitcast(F32)).then_inc(s_wst, 16)

            def store_half(kind, half):
                cols = slice(half * HALF, (half + 1) * HALF)
                if kind == "k":
                    sp.dma_start(k_split[:, :, cols], kf[:].bitcast(F32)).then_inc(s_kdr, 16)
                else:
                    sp.dma_start(q_split[:, :, cols], qf[:].bitcast(F32)).then_inc(s_qdr, 16)

            def stack_k(b, g):
                sp.wait_ge(s_kdr, 16 * 2 * (b * G + g + 1))
                apart(sp)
                for r in range(ROWS4):
                    sp.dma_start(k_stack[r * HD:(r + 1) * HD, g % 2].bitcast(F32),
                                 k_split[:, r % 2, :].rearrange("(h d) n -> d h n", d=HD)).then_inc(s_kst, 16)

            def stack_q(b, g, half):
                cols = slice(half * HALF, (half + 1) * HALF)
                if g:
                    sp.wait_ge(s_qk, b * U + (g - 1) * UPG + (half + 1) * UPG // 2)
                    apart(sp)
                sp.wait_ge(s_qdr, 16 * (2 * (b * G + g) + half + 1))
                apart(sp)
                for r in range(ROWS4):
                    sp.dma_start(q_stack[r * HD:(r + 1) * HD, :, cols].bitcast(F32),
                                 q_split[:, r // 2, cols].rearrange("(h d) n -> d h n", d=HD)
                                 ).then_inc(s_qst[half], 16)

            def load_x(b, t):
                sp.dma_start(x_ln[:, t % 2, :], x[b, t * P:(t + 1) * P, :]).then_inc(s_x[t % 2], 16)

            def reload_x(xb, t):
                sp.wait_ge(s_bn, xb * NT + t + 1)
                apart(sp)
                load_x(xb, (t + 2) % NT)

            def load_adj(b, t):
                sp.dma_start(adj_sb[:, t % 2, :], adj[b, t * P:(t + 1) * P, :]).then_inc(s_adj[t % 2], 16)

            def store_heads(b, n):
                cols = slice((n % 4) * 2 * P, (n % 4 + 1) * 2 * P)
                sp.wait_ge(s_ohi, b * NP + n + 1)
                apart(sp)
                sp.wait_ge(s_olo, b * NP + n + 1)
                apart(sp)
                sp.dma_start(o_split[:, n // 4 % G, :, cols].rearrange("s p n -> p s n"),
                             o_hl[:].bitcast(F32)).then_inc(s_ost, 16)

            def load_out_inputs(b, t):
                rows = slice(t * P, (t + 1) * P)
                if t >= 2:
                    sp.wait_ge(s_y[t % 2], 16 * (b * (NT // 2) + t // 2))
                    apart(sp)
                sp.dma_start(x_res[:, t % 2, :], x[b, rows, :]).then_inc(s_xr[t % 2], 16)
                sp.wait_ge(s_ost, 16 * (b * NP + (G - 1) * 4 + t // 2 + 1))
                apart(sp)
                for part in (HI, LO):
                    sp.dma_start(o_in[:, t % 2, part].bitcast(F32), o_split[part, :, :, rows].rearrange("g p n -> p g n")
                                 ).then_inc(s_oin[t % 2], 16)

            def after_piece(b, pieces, n, kind, g, i):
                done = before(b, pieces) + n + 1
                if kind == "ln" and i + 2 < NT:
                    sp.wait_ge(s_piece, done)
                    apart(sp)
                    load_x(b + g // G, i + 2)
                if kind in ("k", "q"):
                    if g:
                        sp.wait_ge(s_kst if kind == "k" else s_qst[i], 16 * ROWS4 * (b * G + g))
                        apart(sp)
                    sp.wait_ge(s_evac, done)
                    apart(sp)
                    store_half(kind, i)
                if kind in WEIGHTS and i == 1:
                    load = weight_load(kind, g) + 2
                    if pieces is not END or load < G * len(WEIGHTS):
                        sp.wait_ge(s_piece, done)
                        apart(sp)
                        load_weights(load)
                if kind == "out":
                    sp.wait_ge(s_evac, done)
                    apart(sp)
                    sp.dma_start(y[b, i * P:(i + 1) * P, :], x_res[:, i % 2, :]).then_inc(s_y[i % 2], 16)

            load_x(0, 0)
            load_x(0, 1)
            for i, w in enumerate(w_dram):
                sp.dma_start(w_raw[:, i], w.rearrange("(o p) d -> p o d", p=P)).then_inc(s_wload[i], 16)
                for t in (2 * i, 2 * i + 1):
                    reload_x(0, t)
            for n, _, kind, g, i in before_units():
                if kind == "ln" and i % 2 == 0 and i // 2 < len(WEIGHTS):
                    store_split_weights(i // 2)
                if (kind, i) == ("ln", NT - 2):
                    sp.wait_ge(s_wst, 16 * len(WEIGHTS) * G)
                    load_weights(0)
                    load_weights(1)
                    load_adj(0, 0)
                after_piece(0, FIRST, n, kind, g, i)
                if kind == "q":
                    stack_q(0, 0, i)
                elif (kind, i) == ("k", 1):
                    stack_k(0, 0)

            def slots_of(b, slots, pieces):
                last = pieces is END
                for u in slots:
                    g, s = divmod(u, UPG)
                    if s % HPG == 0 and (u // HPG + 1 < NT * G or not last):
                        t = u // HPG + 1
                        if u:
                            sp.wait_ge(s_max, b * U + u)
                            apart(sp)
                        load_adj(b + t // (NT * G), t % NT)
                    if u > slots[0]:
                        for n, _, kind, pg, i in finished_at(pieces, u - 1):
                            after_piece(b, pieces, n, kind, pg, i)
                    if not last or g + 1 < G:
                        if s == STACK_Q[g % G]:
                            stack_q(b, g + 1, 0)
                        if s == STACK_K[g % G]:
                            stack_k(b, g + 1)
                        if s == UPG - 1:
                            stack_q(b, g + 1, 1)
                    for n in product_at(3, u, pieces):
                        store_heads(b, n)
                    if pieces is SIDE:
                        if u in (STATS - 3, STATS - 2):
                            load_x(b + 1, u - STATS + 3)
                        if u - 1 in range(STATS, STATS_END, STATS_STEP):
                            reload_x(b + 1, (u - STATS) // STATS_STEP)
                    for t, at in enumerate(OUT_LOADS):
                        if u == LAST + at:
                            load_out_inputs(b, t)
                for n, _, kind, pg, i in finished_at(pieces, slots[-1]):
                    after_piece(b, pieces, n, kind, pg, i)
                if pieces is not FIRST:
                    for i in range(2):
                        sp.wait_ge(s_y[i], 16 * (b * (NT // 2) + NT // 2))
                        apart(sp)

            slots_of(0, range(BEGIN), FIRST)
            with sp.Fori(0, B - 1) as b:
                slots_of(b, range(BEGIN, U + BEGIN), SIDE)
            slots_of(B - 1, range(BEGIN, U + BEGIN), END)

        @block.gpsimd
        def _(pool):
            def rstd_step(k, step):
                if step == 0:
                    pool.wait_ge(s_guess, k + 1)
                done = (k * NEWTON + step) * 4
                if step:
                    pool.wait_ge(s_newton, done)
                if step < NEWTON:
                    pool.tensor_tensor(newton, rstd, rstd, ALU.mult).then_inc(s_newton, 1)
                    pool.wait_ge(s_newton, done + 1)
                    pool.tensor_tensor(newton, newton, var_eps, ALU.mult).then_inc(s_newton, 1)
                    pool.wait_ge(s_newton, done + 2)
                    apart(pool)
                    pool.tensor_scalar(newton, newton, -0.5, 1.5, ALU.mult, ALU.add).then_inc(s_newton, 1)
                    pool.wait_ge(s_newton, done + 3)
                    pool.tensor_tensor(rstd, rstd, newton, ALU.mult).then_inc(s_newton, 1)
                else:
                    pool.tensor_tensor(shift, mean_var[:, :, 0], rstd, ALU.mult).then_inc(s_shifting, 1)
                    pool.wait_ge(s_shifting, k + 1)
                    apart(pool)
                    pool.tensor_scalar(shift, shift, -1.0, 0.0, ALU.mult, ALU.add).then_inc(s_shift, 1)

            def halve_first(b, u):
                pool.wait_ge(s_max, b * U + u + 1)
                if u >= 2:
                    pool.wait_ge(s_leaf, b * U + u - 1)
                pool.tensor_tensor(tree[:, u % 2, :], neg_a[:, u % 2, 0:512], neg_a[:, u % 2, 512:1024],
                                   ALU.add).then_inc(s_tree1, 1)

            def halve_second(b, u):
                pool.wait_ge(s_tree1, b * U + u + 1)
                pool.tensor_tensor(tree[:, u % 2, 0:256], tree[:, u % 2, 0:256], tree[:, u % 2, 256:512],
                                   ALU.add).then_inc(s_tree2, 1)

            def halve_last(b, u):
                pool.wait_ge(s_tree2, b * U + u + 1)
                if u % PAIR == 0:
                    pool.wait_ge(s_leafsum, b * NP + u // PAIR + 1)
                pool.tensor_tensor(leaf[:, u % PAIR, :], tree[:, u % 2, 0:128], tree[:, u % 2, 128:256],
                                   ALU.add).then_inc(s_leaf, 1)

            pool.sem_inc(s_leafsum, 1)
            pool.memset(ident[:], 0.0).then_inc(s_zero, 1)
            pool.wait_ge(s_zero, 1)
            pool.affine_select(out=ident[:], in_=ident[:], compare_op=ALU.not_equal, fill=1.0, base=0,
                               pattern=[[-1, P]], channel_multiplier=1).then_inc(s_ident, 1)
            for step in range(NEWTON + 1):
                rstd_step(0, step)

            def slots_of(b, slots, pieces):
                for u in slots:
                    for w in units_of(pieces, [u]):
                        halve_first(b, w)
                    for w in units_of(pieces, [u - 1] if u else []):
                        halve_last(b, w)
                    for w in units_of(pieces, [u]):
                        halve_second(b, w)
                    if u in range(STATS_END - 1, STATS_END + NEWTON) and pieces is SIDE:
                        rstd_step(b + 1, u - STATS_END + 1)

            slots_of(0, range(BEGIN), FIRST)
            with pool.Fori(0, B - 1) as b:
                slots_of(b, range(BEGIN, U + BEGIN), SIDE)
            slots_of(B - 1, range(BEGIN, U + 1), END)

        @block.tensor
        def _(pe):
            def scores(b, u):
                g, t, h = unit(u)
                if u >= 2:
                    pe.wait_ge(s_max, b * U + u - 1)
                if u % UPG == 0:
                    pe.wait_ge(s_kst, 16 * ROWS4 * (b * G + g + 1))
                    pe.wait_ge(s_qst[0], 16 * ROWS4 * (b * G + g + 1))
                if u % UPG == UPG // 2:
                    pe.wait_ge(s_qst[1], 16 * ROWS4 * (b * G + g + 1))
                for half in range(2):
                    mm = pe.matmul(ps[:, 2 * (u % 2) + half, :], q_stack[:, h, t * P:(t + 1) * P],
                                   k_stack[:, g % 2, h, half * HALF:(half + 1) * HALF], start=True, stop=True)
                mm.then_inc(s_qk, 1)

            def turn_probs(b, u):
                pe.wait_ge(s_exp, b * U + u + 1)
                for half in range(2):
                    if u:
                        pe.wait_ge(s_copy[half], b * U + u)
                    for c in range(4):
                        mm = pe.transpose(ps[:, 4 + half, c * P:(c + 1) * P],
                                          prob[:, u % 2, (4 * half + c) * P:(4 * half + c + 1) * P], ident[:])
                    mm.then_inc(s_turn, 1)

            def times_v(b, n, pieces):
                g = n // 4
                if n:
                    pe.wait_ge(s_norm, b * NP + n)
                pe.wait_ge(s_copy[0], b * U + PAIR * (n + 1))
                pe.wait_ge(s_copy[1], b * U + PAIR * (n + 1))
                if n % 4 == 0:
                    pe.wait_ge(s_evac, before(b, pieces) + number(pieces, "vt", g, 1) + 1)
                for c in range(MC):
                    for h in range(HPG):
                        mm = pe.matmul(ps[h * HD:(h + 1) * HD, 6, 0:2 * P], v_sb[:, g % 2, c, h * HD:(h + 1) * HD],
                                       probT[:, h, c, :], start=(c == 0), stop=(c == MC - 1))
                    if c == MC // 2 - 1:
                        mm.then_inc(s_pv1, 1)
                mm.then_inc(s_pv, 1)

            def turn_rec(b, n):
                pe.wait_ge(s_rr, b * NP + n + 1)
                for j in range(2):
                    mm = pe.transpose(rec_out[:, j * P:(j + 1) * P],
                                      rec_rep[:, j].rearrange("p h d -> p (h d)"), ident[:])
                mm.then_inc(s_rt, 1)

            def piece(b, pieces, n, part, parts, kind, g, i):
                if part == 0 and (n or pieces is not FIRST):
                    pe.wait_ge(s_evac, before(b, pieces) + n)
                steps = [(c, p) for c in range(DC) for p in PRODUCTS]
                here = range(part * len(steps) // parts, (part + 1) * len(steps) // parts)
                if kind in WEIGHTS:
                    load = weight_load(kind, g)
                    if i == 0 and part == 0:
                        pe.wait_ge(s_wp[load % 2], 16 * (b * (G * len(WEIGHTS) // 2) + load // 2 + 1))
                    for k in here:
                        c, (pw, ph) = steps[k]
                        mm = pe.matmul(side_bank, w_proj[:, load % 2, pw, c, :], hT[ph][:, c, i * HALF:(i + 1) * HALF],
                                       start=(k == 0), stop=(k == len(steps) - 1))
                elif kind == "vt":
                    for c in range(4):
                        mm = pe.transpose(side_bank[:, c * P:(c + 1) * P], vTh[:, c * P:(c + 1) * P], ident[:])
                elif kind == "ln":
                    pe.wait_ge(s_xn, (b + g // G) * NT + i + 1)
                    for c in range(DC):
                        mm = pe.transpose(side_bank[:, c * P:(c + 1) * P], x_ln[:, i % 2, c * P:(c + 1) * P], ident[:])
                else:
                    if part == 0:
                        pe.wait_ge(s_oin[i % 2], 32 * (b * (NT // 2) + i // 2 + 1))
                    for k in here:
                        c, (pw, po) = steps[k]
                        mm = pe.matmul(side_bank, o_in[:, i % 2, po, c, :], w_out[:, pw, c, :],
                                       start=(k == 0), stop=(k == len(steps) - 1))
                if part == parts - 1:
                    mm.then_inc(s_piece, 1)

            pe.wait_ge(s_ident, 1)
            for k in range(4 * DC):
                w, ic = divmod(k, DC)
                if ic == 0:
                    pe.wait_ge(s_wload[w], 16)
                if k >= 4:
                    pe.wait_ge(s_wlo, k - 3)
                for oc in range(DC):
                    mm = pe.transpose(ps[:, k % 4, oc * P:(oc + 1) * P],
                                      w_raw[:, w, oc, ic * P:(ic + 1) * P], ident[:])
                mm.then_inc(s_wt, 1)
            pe.wait_ge(s_wlo, 4 * DC)
            for n, _, kind, g, i in before_units():
                piece(0, FIRST, n, 0, 1, kind, g, i)

            def slots_of(b, slots, pieces):
                for u in slots:
                    ahead, further = scores_in(u, pieces)
                    for w in ahead:
                        scores(b, w)
                    for w in units_of(pieces, [u]):
                        turn_probs(b, w)
                    for w in further:
                        scores(b, w)
                    for n in product_at(0, u, pieces):
                        times_v(b, n, pieces)
                        turn_rec(b, n)
                    for n, part, parts, kind, g, i in parts_at(pieces, u):
                        piece(b, pieces, n, part, parts, kind, g, i)

            for u in range(LEAD):
                scores(0, u)
            slots_of(0, range(BEGIN), FIRST)
            with pe.Fori(0, B - 1) as b:
                slots_of(b, range(BEGIN, U + BEGIN), SIDE)
            slots_of(B - 1, range(BEGIN, U + BEGIN), END)

        @block.scalar
        def _(act):
            def probs(b, u):
                n = u // PAIR
                act.wait_ge(s_max, b * U + u + 1)
                if u >= 2:
                    act.wait_ge(s_turn, (b * U + u - 1) * 2)
                act.activation(prob[:, u % 2, :], neg_a[:, u % 2, :], ACT.Exp,
                               bias=neg_max[:, n % 2, u % PAIR:u % PAIR + 1], scale=-1.0,
                               accum_out=row_sum[:, n % 2, u % PAIR:u % PAIR + 1]).then_inc(s_exp, 1)

            def copy_turned(b, u):
                _, t, h = unit(u)
                act.wait_ge(s_turn, (b * U + u) * 2 + 1)
                if u >= PAIR:
                    act.wait_ge(s_pv1, b * NP + u // PAIR)
                act.copy(probT[:, h, 0:4, (t % 2) * P:(t % 2 + 1) * P],
                         ps[:, 4, :].rearrange("p (c n) -> p c n", n=P)).then_inc(s_copy[0], 1)

            def evacuate(b, pieces, n, m, kind, g, i):
                if kind == "out":
                    return
                act.wait_ge(s_piece, before(b, pieces) + n + 1)
                if kind == "k":
                    if g or i:
                        act.wait_ge(s_kdr, 16 * ((b * G + g) * 2 + i))
                    act.copy(kf[:, HI, :], side_bank).then_inc(s_hi, 1)
                elif kind == "q":
                    if g or i:
                        act.wait_ge(s_qdr, 16 * ((b * G + g) * 2 + i))
                    act.mul(qf[:, HI, :], side_bank, QSCALE).then_inc(s_hi, 1)
                elif kind == "v":
                    act.copy(vTh[:], side_bank).then_inc(s_evac, 1)
                elif kind == "vt":
                    act.copy(v_sb[:, g % 2, 4 * i:4 * i + 4, :], side_bank.rearrange("p (c n) -> p c n", n=P)
                             ).then_inc(s_evac, 1)
                else:
                    act.activation(hT[HI][:, :, i * P:(i + 1) * P], side_bank.rearrange("p (c n) -> p c n", n=P),
                                   ACT.Relu).then_inc(s_hi, 1)

            def copy_rec(b, n):
                act.wait_ge(s_rt, b * NP + n + 1)
                if n:
                    act.wait_ge(s_olo, b * NP + n)
                act.copy(o_norm[:], rec_out).then_inc(s_rc, 1)

            def tile_norm(xb, t):
                act.wait_ge(s_x[t % 2], 16 * (NT * xb + NT // 2 + t // 2 + 1))
                act.wait_ge(s_shift, xb + 1)
                act.activation(x_ln[:, t % 2, :], x_ln[:, t % 2, :], ACT.Identity,
                               bias=shift[:, t:t + 1], scale=rstd[:, t:t + 1]).then_inc(s_xn, 1)

            def heads_hi(b, n):
                act.wait_ge(s_norm, b * NP + n + 1)
                if n:
                    act.wait_ge(s_ost, 16 * (b * NP + n))
                act.copy(o_hl[:, HI, :], o_norm[:]).then_inc(s_ohi, 1)

            for k in range(4 * DC):
                w, ic = divmod(k, DC)
                act.wait_ge(s_wt, k + 1)
                act.copy(w_stage[w][:, HI * DC + ic, :], ps[:, k % 4, :]).then_inc(s_whi, 1)
            tile_norm(0, 0)
            for n, m, kind, g, i in before_units():
                if kind == "ln" and i + 1 < NT:
                    tile_norm(0, i + 1)
                evacuate(0, FIRST, n, m, kind, g, i)

            def slots_of(b, slots, pieces):
                for u in slots:
                    if u > slots[0]:
                        for n, m, kind, g, i in finished_at(pieces, u - 1):
                            evacuate(b, pieces, n, m, kind, g, i)
                    if not beside_product(u - 1):
                        for w in units_of(pieces, [u + 1]):
                            probs(b, w)
                    if beside_product(u):
                        for w in units_of(pieces, [u + 2]):
                            probs(b, w)
                    for n in product_at(1, u, pieces):
                        copy_rec(b, n)
                    for w in units_of(pieces, [u]):
                        copy_turned(b, w)
                    for n in product_at(1, u, pieces):
                        heads_hi(b, n)
                    for _, _, _, kind, g, i in parts_at(pieces, u + 1):
                        if kind == "ln":
                            tile_norm(b + g // G, i)
                for n, m, kind, g, i in finished_at(pieces, slots[-1]):
                    evacuate(b, pieces, n, m, kind, g, i)

            probs(0, 0)
            slots_of(0, range(BEGIN), FIRST)
            with act.Fori(0, B - 1) as b:
                slots_of(b, range(BEGIN, U + BEGIN), SIDE)
            slots_of(B - 1, range(BEGIN, U + BEGIN), END)

        @block.vector
        def _(dve):
            def bias_and_max(b, u):
                _, t, _ = unit(u)
                n = u // PAIR
                tile = u // HPG
                dve.wait_ge(s_qk, b * U + u + 1)
                if u % HPG == 0:
                    dve.wait_ge(s_adj[tile % 2], 16 * (b * (G * NT // 2) + tile // 2 + 1))
                if u >= 2:
                    dve.wait_ge(s_exp, b * U + u - 1)
                    dve.wait_ge(s_tree1, b * U + u - 1)
                apart(dve)
                dve.tensor_tensor_reduce(
                    neg_a[:, u % 2, :], ps[:, 2 * (u % 2):2 * (u % 2) + 2, :].rearrange("p h m -> p (h m)"),
                    adj_sb[:, tile % 2, :], -2.0, 3.0e38, ALU.add, ALU.min,
                    neg_max[:, n % 2, u % PAIR:u % PAIR + 1]).then_inc(s_max, 1)

            def copy_turned(b, u):
                _, t, h = unit(u)
                dve.wait_ge(s_turn, (b * U + u) * 2 + 2)
                if u >= PAIR:
                    dve.wait_ge(s_pv, b * NP + u // PAIR)
                dve.tensor_copy(probT[:, h, 4:8, (t % 2) * P:(t % 2 + 1) * P],
                                ps[:, 5, :].rearrange("p (c n) -> p c n", n=P)).then_inc(s_copy[1], 1)

            def reciprocals(b, n):
                steps = (b * NP + n) * 4
                dve.wait_ge(s_leaf, b * U + PAIR * (n + 1))
                dve.wait_ge(s_exp, b * U + PAIR * (n + 1))
                dve.tensor_reduce(neg_sum[:], leaf[:], AX.X, ALU.add).then_inc(s_leafsum, 1)
                dve.reciprocal(rec_sum[:], row_sum[:, n % 2]).then_inc(s_rstep, 1)
                dve.tensor_scalar(nonzero[:], neg_max[:, n % 2], 0.0, None, ALU.not_equal).then_inc(s_rstep, 1)
                dve.wait_ge(s_leafsum, b * NP + n + 2)
                dve.wait_ge(s_rstep, steps + 2)
                dve.scalar_tensor_tensor(nonzero[:], neg_sum[:], 0.0, nonzero[:], ALU.not_equal, ALU.max
                                         ).then_inc(s_rstep, 1)
                dve.wait_ge(s_rstep, steps + 3)
                dve.tensor_tensor(rec[:], nonzero[:], rec_sum[:], ALU.mult).then_inc(s_rstep, 1)
                dve.wait_ge(s_rstep, steps + 4)
                dve.tensor_copy(rec_rep[:].rearrange("p j h d -> p (j h) d"),
                                rec[:].unsqueeze(2).to_broadcast([P, PAIR, HD])).then_inc(s_rr, 1)

            def tile_stats(xb, t):
                k = xb * NT + t
                dve.wait_ge(s_x[t % 2], 16 * (NT * xb + t // 2 + 1))
                if t or not isinstance(xb, int):
                    dve.wait_ge(s_mv, k)
                dve.bn_stats(bn, x_ln[:, t % 2, :]).then_inc(s_bn, 1)

            def tile_mean(xb, t):
                dve.wait_ge(s_bn, xb * NT + t + 1)
                apart(dve)
                dve.bn_aggr(mean_var[:, t, :], bn).then_inc(s_mv, 1)

            def rstd_guess(xb):
                dve.wait_ge(s_mv, (xb + 1) * NT)
                dve.tensor_scalar(var_eps, mean_var[:, :, 1], EPS, None, ALU.add).then_inc(s_ve, 1)
                dve.wait_ge(s_ve, xb + 1)
                dve.tensor_scalar(rstd.bitcast(I32), var_eps.bitcast(I32), -0.5, RSQRT_BITS,
                                  ALU.mult, ALU.add).then_inc(s_guess, 1)

            def evacuate(b, pieces, n, m, kind, g, i):
                if kind in ("v", "vt"):
                    return
                dve.wait_ge(s_piece, before(b, pieces) + n + 1)
                if kind in SPLIT:
                    dve.wait_ge(s_hi, splits_before(b, pieces) + m + 1)
                side_c = side_bank.rearrange("p (c n) -> p c n", n=P)
                if kind == "k":
                    op = dve.scalar_tensor_tensor(kf[:, LO, :], side_bank, 1.0, kf[:, HI, :].bitcast(F32),
                                                  ALU.mult, ALU.subtract)
                elif kind == "q":
                    op = dve.scalar_tensor_tensor(qf[:, LO, :], side_bank, QSCALE, qf[:, HI, :].bitcast(F32),
                                                  ALU.mult, ALU.subtract)
                elif kind == "ln":
                    rows = slice(i * P, (i + 1) * P)
                    op = dve.scalar_tensor_tensor(hT[LO][:, :, rows], side_c, 0.0, hT[HI][:, :, rows].bitcast(F32),
                                                  ALU.max, ALU.subtract)
                else:
                    dve.wait_ge(s_xr[i % 2], 16 * (b * (NT // 2) + i // 2 + 1))
                    op = dve.tensor_tensor(x_res[:, i % 2, :], side_bank, x_res[:, i % 2, :], ALU.add)
                op.then_inc(s_evac, 1)

            def normalise(b, n):
                dve.wait_ge(s_pv, b * NP + n + 1)
                dve.wait_ge(s_rc, b * NP + n + 1)
                dve.tensor_tensor(o_norm[:], heads_out, o_norm[:], ALU.mult).then_inc(s_norm, 1)

            def heads_lo(b, n):
                dve.wait_ge(s_ohi, b * NP + n + 1)
                dve.tensor_tensor(o_hl[:, LO, :], o_norm[:], o_hl[:, HI, :].bitcast(F32), ALU.subtract
                                  ).then_inc(s_olo, 1)

            for t in range(NT):
                tile_stats(0, t)
                tile_mean(0, t)
            rstd_guess(0)
            for k in range(4 * DC):
                w, ic = divmod(k, DC)
                dve.wait_ge(s_whi, k + 1)
                dve.scalar_tensor_tensor(w_stage[w][:, LO * DC + ic, :], ps[:, k % 4, :], 1.0,
                                         w_stage[w][:, HI * DC + ic, :].bitcast(F32),
                                         ALU.mult, ALU.subtract).then_inc(s_wlo, 1)
            for n, m, kind, g, i in before_units():
                evacuate(0, FIRST, n, m, kind, g, i)

            def slots_of(b, slots, pieces):
                for u in slots:
                    ahead, further = scores_in(u, pieces)
                    if u > slots[0]:
                        for n, m, kind, g, i in finished_at(pieces, u - 1):
                            evacuate(b, pieces, n, m, kind, g, i)
                    for w in ahead:
                        bias_and_max(b, w)
                    for n in product_at(2, u, pieces):
                        heads_lo(b, n)
                    for n in product_at(1, u, pieces):
                        normalise(b, n)
                    for n in product_at(0, u, pieces):
                        reciprocals(b, n)
                    for w in further:
                        bias_and_max(b, w)
                    for w in units_of(pieces, [u]):
                        copy_turned(b, w)
                    if pieces is SIDE:
                        if u in range(STATS, STATS_END, STATS_STEP):
                            tile_stats(b + 1, (u - STATS) // STATS_STEP)
                        if u - 1 in range(STATS, STATS_END, STATS_STEP):
                            tile_mean(b + 1, (u - STATS) // STATS_STEP)
                        if u == STATS_END - 2:
                            rstd_guess(b + 1)
                for n, m, kind, g, i in finished_at(pieces, slots[-1]):
                    evacuate(b, pieces, n, m, kind, g, i)

            for u in range(LEAD):
                bias_and_max(0, u)
            slots_of(0, range(BEGIN), FIRST)
            with dve.Fori(0, B - 1) as b:
                slots_of(b, range(BEGIN, U + BEGIN), SIDE)
            slots_of(B - 1, range(BEGIN, U + BEGIN), END)


_INS = ["x", "adj", "L0_gnn_Wq", "L0_gnn_Wk", "L0_gnn_Wv", "L0_gnn_Wo"]


def kernel(**inputs):
    import concourse.bacc as bacc
    from concourse.bass_utils import run_bass_kernel_spmd

    nc = bacc.Bacc("TRN2", target_bir_lowering=False, num_devices=1)
    arrays, args = {}, []
    for name in _INS:
        a = np.ascontiguousarray(inputs[name])
        arrays[f"in_{name}"] = a
        args.append(nc.dram_tensor(f"in_{name}", a.shape, mybir.dt.from_np(a.dtype), kind="ExternalInput").ap())
    out = nc.dram_tensor("out_y", (B, N, D), F32, kind="ExternalOutput").ap()
    adj_attention_block(nc, *args, out)
    r = run_bass_kernel_spmd(nc, [arrays], core_ids=[0])
    return r.results[0]["out_y"]
```
